# Optimizing a Trainium2 kernel written in Bass

```python
import numpy as np
import jax
import jax.numpy as jnp

def _softmax(x, axis=-1):
    return jax.nn.softmax(x, axis=axis)

def _gelu(x):
    return jax.nn.gelu(x, approximate=True)

def _silu(x):
    return jax.nn.silu(x)

def _sigmoid(x):
    return jax.nn.sigmoid(x)

def _layernorm(x, axis=-1, eps=1e-05):
    m = jnp.mean(x, axis=axis, keepdims=True)
    v = jnp.var(x, axis=axis, keepdims=True)
    return (x - m) / jnp.sqrt(v + eps)

def _scatter_add(tgt, idx, src, axis=0):
    return tgt.at[idx].add(src)

def _segment_sum(src, seg, n):
    return jax.ops.segment_sum(src, seg, n)
kernel_name = 'mk_macaron_d1_jaxref_r8_f661d2'

def setup_inputs(seed: int=0):
    np.random.seed(seed)
    _w = jnp.asarray

    def _L0_attn_setup():
        import jax, jax.numpy as jnp
        import numpy as np
        W_SEG = 256
        R = 4
        H = 16
        key = jax.random.key(seed)
        k0, k1, k2 = jax.random.split(key, 3)
        B, S, Hid = (2, 1024, 128)
        X = jax.random.normal(k0, (B, S, Hid), dtype=jnp.float32)
        Wq = jax.random.normal(k1, (Hid, Hid), dtype=jnp.float32) * 0.02
        bq = jnp.zeros((Hid,), jnp.float32)
        Wkv = jax.random.normal(k2, (Hid, 2 * Hid), dtype=jnp.float32) * 0.02
        bkv = jnp.zeros((2 * Hid,), jnp.float32)
        return {'X': X, 'Wq': Wq, 'bq': bq, 'Wkv': Wkv, 'bkv': bkv}
    _L0_attn_in = _L0_attn_setup()

    def _L0_ffn_setup():
        import jax, jax.numpy as jnp
        import numpy as np
        B, S, D, H, E = (4, 256, 128, 512, 8)
        key = jax.random.key(seed)
        ks = jax.random.split(key, 8)
        s_d = 1.0 / np.sqrt(D)
        s_h = 1.0 / np.sqrt(H)
        return {'x': jax.random.normal(ks[0], (B, S, D), dtype=jnp.float32), 'gate_w': jax.random.uniform(ks[1], (E, D), jnp.float32, -s_d, s_d), 'gate_b': jax.random.uniform(ks[2], (E,), jnp.float32, -s_d, s_d), 'w1': jax.random.uniform(ks[3], (E, H, D), jnp.float32, -s_d, s_d), 'b1': jax.random.uniform(ks[4], (E, H), jnp.float32, -s_d, s_d), 'w2': jax.random.uniform(ks[5], (E, D, H), jnp.float32, -s_h, s_h), 'b2': jax.random.uniform(ks[6], (E, D), jnp.float32, -s_h, s_h)}
    _L0_ffn_in = _L0_ffn_setup()
    _d = {'L0_attn_X': _L0_attn_in['X'], 'L0_attn_Wq': _L0_attn_in['Wq'], 'L0_attn_bq': _L0_attn_in['bq'], 'L0_attn_Wkv': _L0_attn_in['Wkv'], 'L0_attn_bkv': _L0_attn_in['bkv'], 'L0_ffn_gate_w': _L0_ffn_in['gate_w'], 'L0_ffn_gate_b': _L0_ffn_in['gate_b'], 'L0_ffn_w1': _L0_ffn_in['w1'], 'L0_ffn_b1': _L0_ffn_in['b1'], 'L0_ffn_w2': _L0_ffn_in['w2'], 'L0_ffn_b2': _L0_ffn_in['b2']}
    _x0 = _d['L0_attn_X']
    _d['L0_attn_X'] = jax.random.normal(jax.random.fold_in(jax.random.key(seed), 1), (32, 256, 128), dtype=_x0.dtype)
    del _x0
    return _d

def reference(L0_attn_X, L0_attn_Wq, L0_attn_bq, L0_attn_Wkv, L0_attn_bkv, L0_ffn_gate_w, L0_ffn_gate_b, L0_ffn_w1, L0_ffn_b1, L0_ffn_w2, L0_ffn_b2):

    def _L0_attn_ref(X, Wq, bq, Wkv, bkv):
        import jax, jax.numpy as jnp
        import numpy as np
        W_SEG = 256
        R = 4
        H = 16
        B, S, Hid = X.shape
        D = Hid // H
        num_points = W_SEG // R
        num_seg = S // W_SEG
        scale = 1.0 / np.sqrt(D).astype(np.float32)
        q = (X @ Wq + bq).reshape(B, S, H, D)
        kv = (X @ Wkv + bkv).reshape(B, S, 2, H, D)
        k, v = (kv[:, :, 0], kv[:, :, 1])
        base = (jnp.arange(num_seg)[:, None] * W_SEG + jnp.arange(num_points)[None, :] * R).reshape(-1)
        shift = jnp.arange(H) % R
        idx = base[None, :] + shift[:, None]
        Tq = idx.shape[1]
        idxT = idx.T
        head_ix = jnp.arange(H)[None, :]
        sq = q[:, idxT, head_ix, :]
        sk = k[:, idxT, head_ix, :]
        sv = v[:, idxT, head_ix, :]
        sq = sq.reshape(B, num_seg, num_points, H, D)
        sk = sk.reshape(B, num_seg, num_points, H, D)
        sv = sv.reshape(B, num_seg, num_points, H, D)
        scores = jnp.einsum('bsqhd,bskhd->bshqk', sq, sk) * scale
        probs = jax.nn.softmax(scores, axis=-1)
        ctx = jnp.einsum('bshqk,bskhd->bsqhd', probs, sv)
        ctx = ctx.reshape(B, Tq, H, D)
        out = jnp.zeros((B, S, H, D), ctx.dtype).at[:, idxT, head_ix, :].set(ctx)
        return out.reshape(B, S, Hid)

    def _L0_ffn_ref(x, gate_w, gate_b, w1, b1, w2, b2):
        import jax, jax.numpy as jnp
        import numpy as np
        B, S, D, H, E = (4, 256, 128, 512, 8)
        b, s, d = x.shape
        xf = x.reshape(-1, d)
        logits = xf @ gate_w.T + gate_b
        top1 = jnp.argmax(logits, axis=-1)
        out = jnp.zeros_like(xf)
        n_experts = w1.shape[0]
        for e in range(n_experts):
            h = jax.nn.relu(xf @ w1[e].T + b1[e])
            y = h @ w2[e].T + b2[e]
            out = out + jnp.where((top1 == e)[:, None], y, jnp.zeros((), y.dtype))
        return out.reshape(b, s, d)
    x = L0_attn_X
    x = x + 0.5 * _L0_ffn_ref(_layernorm(x, axis=-1), L0_ffn_gate_w, L0_ffn_gate_b, L0_ffn_w1, L0_ffn_b1, L0_ffn_w2, L0_ffn_b2)
    x = x + _L0_attn_ref(_layernorm(x, axis=-1), L0_attn_Wq, L0_attn_bq, L0_attn_Wkv, L0_attn_bkv)
    x = x + 0.5 * _L0_ffn_ref(_layernorm(x, axis=-1), L0_ffn_gate_w, L0_ffn_gate_b, L0_ffn_w1, L0_ffn_b1, L0_ffn_w2, L0_ffn_b2)
    return x

_drawn_inputs = setup_inputs


def setup_inputs(seed=0):
    import zlib

    import numpy as np

    out = dict(_drawn_inputs(seed))
    spreads = {'L0_attn_bq': (0.0, 0.8), 'L0_attn_bkv': (0.0, 0.1)}
    factors = {'L0_attn_Wq': 8.0, 'L0_attn_Wkv': 2.919}
    for name, (base, spread) in spreads.items():
        noise = np.random.default_rng([zlib.crc32(name.encode()), seed]).standard_normal(out[name].shape)
        drawn = base * np.exp(spread * noise) if base else spread * noise
        out[name] = jnp.asarray(drawn.astype(out[name].dtype))
    for name, factor in factors.items():
        out[name] = (out[name] * factor).astype(out[name].dtype)
    return out
```

```python
from contextlib import ExitStack

import numpy as np

import concourse.bass as bass
from concourse import mybir

ALU = mybir.AluOpType
ACT = mybir.ActivationFunctionType
AX = mybir.AxisListType
F32 = mybir.dt.float32
BF16 = mybir.dt.bfloat16
I32 = mybir.dt.int32
U32 = mybir.dt.uint32

P = 128
HEADS, HEAD_DIM, R = 16, 8, 4
CLASS_HEADS = HEADS // R
CLASS_CH = CLASS_HEADS * HEAD_DIM
ROWS = CLASS_HEADS // 2

C_IDENT, C_TRI, C_IOTA, C_LOWER, C_HEAD, C_END = 0, 128, 256, 264, 336, 340


def shape_constants(experts):
    c = np.zeros((P, C_END), np.float32)
    k = np.arange(P)
    c[:, C_IDENT:C_IDENT + P] = k[:, None] == k[None, :]
    c[:, C_TRI:C_TRI + P] = k[:, None] < k[None, :]
    e = np.arange(experts)
    c[:, C_IOTA:C_IOTA + experts] = e - experts
    c[:, C_LOWER:C_LOWER + (experts + 1) * experts] = (e[None, :] < np.arange(experts + 1)[:, None]).reshape(1, -1)
    c[:, C_HEAD:C_HEAD + CLASS_HEADS] = (k[:, None] % CLASS_CH) // HEAD_DIM == np.arange(CLASS_HEADS)[None, :]
    return c


def macaron_kernel(nc, x, w_qkv, b_qkv, gate_w, gate_b, w1, b1, w2, b2, consts, out):
    TOKENS, D = x.shape
    E = gate_w.shape[1]
    HID = w1.shape[2]
    HC = HID // P
    CHUNKS = TOKENS // (P * R)
    GROUPS = 2
    CPG = CHUNKS // GROUPS
    TG = CPG * R
    HALVES = 2
    ST = HALVES * P
    SEQ = P // 2
    MAX_TILES = TG * P // ST + E
    ROWS_CAP = (MAX_TILES + 2) * ST
    EPS = 1e-5
    FILLS, SPARES = 4, 2
    FILL = ROWS_CAP * D // P // FILLS
    SCALE = float(1.0 / np.sqrt(HEAD_DIM))
    QKV = 3 * CLASS_CH

    sorted_in = [nc.dram_tensor(f"sorted_in{g}", (ROWS_CAP, D), F32, kind="Internal").ap() for g in range(GROUPS)]
    sorted_out = [nc.dram_tensor(f"sorted_out{g}", (MAX_TILES * ST, D), F32, kind="Internal").ap() for g in range(GROUPS)]
    MIN_TILES = TG * P // ST
    x_chunks = x.rearrange("(c p r) d -> p c (r d)", p=P, r=R)
    out_chunks = out.rearrange("(c p r) d -> p c (r d)", p=P, r=R)

    with ExitStack() as ctx:
        def sb(name, shape, dt=F32):
            return ctx.enter_context(nc.sbuf_tensor(name, shape, dt))

        def sem(name):
            return ctx.enter_context(nc.semaphore(name))

        bank = [ctx.enter_context(nc.psum_tensor(f"bank{i}", [P, 512], F32)) for i in range(8)]

        cst = sb("cst", [P, C_END])
        ident = cst[:, C_IDENT:C_IDENT + P]
        expert_iota = cst[:, C_IOTA:C_IOTA + E]
        lower = cst[:, C_LOWER:C_LOWER + (E + 1) * E].rearrange("p (i e) -> p i e", e=E)
        head_mask = cst[:, C_HEAD:C_HEAD + CLASS_HEADS]
        tri = sb("tri", [P, P], BF16)
        ones = sb("ones", [P, P], BF16)
        w1_sb = sb("w1_sb", [P, E, HID])
        w2_sb = sb("w2_sb", [P, E, HC, D])
        b1_sb = sb("b1_sb", [P, E * HC])
        b2_sb = sb("b2_sb", [P, E, D])
        gate_sb = sb("gate_sb", [P, E])
        gate_b_sb = sb("gate_b_sb", [P, E])
        wqkv_sb = sb("wqkv_sb", [P, R, QKV])
        bqkv_sb = sb("bqkv_sb", [P, R, QKV])
        x_sb = sb("x_sb", [P, CHUNKS, R * D])
        xn_sb = sb("xn_sb", [P, CHUNKS, R, D])
        stats = sb("stats", [P, TG, 6])
        mean = sb("mean", [P, TG])
        var = sb("var", [P, TG])
        diff = sb("diff", [P, TG])
        m2 = sb("m2", [P, TG])
        std = sb("std", [P, TG])
        rstd = sb("rstd", [P, TG])
        xnT = sb("xnT", [P, 2, R, P])
        logits = sb("logits", [P, TG, E])
        top = sb("top", [P, TG])
        hit = sb("hit", [P, TG, E])
        first = sb("first", [P, TG])
        onehot = sb("onehot", [P, TG, E], BF16)
        scan = [sb(f"scan{i}", [P, E, TG]) for i in range(2)]
        place = sb("place", [P, TG, E])
        tiles_i = sb("tiles_i", [P, E], I32)
        tiles_f = sb("tiles_f", [P, E])
        starts_m = sb("starts_m", [P, E + 1, E])
        starts_f = sb("starts_f", [P, E + 1])
        starts = [sb(f"starts{g}", [P, E + 1], I32) for g in range(GROUPS)]
        rows_f = sb("rows_f", [P, TG])
        rows = [sb(f"rows{g}", [P, TG], U32) for g in range(GROUPS)]
        zeros = sb("zeros", [P, FILL])
        x_in = sb("x_in", [P, HALVES, D])
        xT = sb("xT", [P, ST])
        hT = sb("hT", [P, HC, ST])
        y_sb = sb("y_sb", [P, HALVES, D])
        y_back = sb("y_back", [P, 2, R * D])
        qk = sb("qk", [P, 2, R, CLASS_CH])
        q_by_class = sb("q_by_class", [P, R, P])
        k_by_head = sb("k_by_head", [P, CLASS_HEADS, P])
        v_pairs = sb("v_pairs", [P, 2, 2, R, ROWS, 2 * (HEAD_DIM + 1)])
        row_max = sb("row_max", [P, R * CLASS_HEADS])
        probs = sb("probs", [P, R, CLASS_HEADS * SEQ])
        probsT = sb("probsT", [P, R * ROWS, P])
        inv_sum = sb("inv_sum", [P, R * CLASS_HEADS])
        attended = sb("attended", [P, R * CLASS_HEADS, HEAD_DIM])

        consts_loaded, weights_loaded = sem("consts_loaded"), sem("weights_loaded")
        XL = 4
        x_loaded = [sem(f"x_loaded{i}") for i in range(XL)]
        experts_loaded = sem("experts_loaded")
        zeros_ready = sem("zeros_ready")
        padded = [sem(f"padded{g}") for g in range(GROUPS)]
        spares_filled = sem("spares_filled")
        v_done = sem("v_done")
        consts_ready = sem("consts_ready")
        var_ready, std_ready = sem("var_ready"), sem("std_ready")
        xn_ready = sem("xn_ready")
        xnT_done, xnT_copied = sem("xnT_done"), sem("xnT_copied")
        logits_done, onehot_ready, ranks_done = sem("logits_done"), sem("onehot_ready"), sem("ranks_done")
        routed = sem("routed")
        phases = [(f, g) for f in range(2) for g in range(GROUPS)]
        scattered = {k: sem(f"scattered_{k[0]}{k[1]}") for k in phases}
        x_in_loaded = {k: sem(f"x_in_loaded_{k[0]}{k[1]}") for k in phases}
        xT_done = {k: sem(f"xT_done_{k[0]}{k[1]}") for k in phases}
        xT_copied = {k: sem(f"xT_copied_{k[0]}{k[1]}") for k in phases}
        h_done = {k: sem(f"h_done_{k[0]}{k[1]}") for k in phases}
        relu_v = {k: sem(f"relu_v_{k[0]}{k[1]}") for k in phases}
        relu_a = {k: sem(f"relu_a_{k[0]}{k[1]}") for k in phases}
        y_done = {k: sem(f"y_done_{k[0]}{k[1]}") for k in phases}
        y_copied = {k: sem(f"y_copied_{k[0]}{k[1]}") for k in phases}
        y_stored = {k: sem(f"y_stored_{k[0]}{k[1]}") for k in phases}
        experts_done, pe_phases = sem("experts_done"), sem("pe_phases")
        gathered = [sem(f"gathered{i}") for i in range(2)]
        y_back_used = sem("y_back_used")
        qkv_done, qk_ready, v_ready = sem("qkv_done"), sem("qk_ready"), sem("v_ready")
        qT_done, q_ready, kT_done, k_ready = sem("qT_done"), sem("q_ready"), sem("kT_done"), sem("k_ready")
        scores_done, shifted, exp_done = sem("scores_done"), sem("shifted"), sem("exp_done")
        probsT_done, probsT_copied = sem("probsT_done"), sem("probsT_copied")
        ctx_done, ctx_used = sem("ctx_done"), sem("ctx_used")
        x_final, out_stored = sem("x_final"), sem("out_stored")

        block = ctx.enter_context(nc.Block())

        order = [("ffn", 0, 0), ("ffn", 0, 1)] + [(kind, 1, g) for g in range(GROUPS) for kind in ("attn", "ffn")]
        norm_base = {step: i * CPG for i, step in enumerate(order)}
        norm_phase = {step: i for i, step in enumerate(order)}
        route_phase = {(f, g): i for i, (f, g) in enumerate(phases)}

        def expert_bounds(eng, g):
            return [eng.value_load(starts[g][0:1, e:e + 1], min_val=e, max_val=MAX_TILES) for e in range(E + 1)]

        @block.sync
        def _(sp):
            sp.dma_start(cst[:], consts).then_inc(consts_loaded, 16)
            per = CHUNKS // XL
            for i in range(XL):
                sp.dma_start(x_sb[:, i * per:(i + 1) * per, :],
                             x_chunks[:, i * per:(i + 1) * per, :]).then_inc(x_loaded[i], 16)
            sp.wait_ge(zeros_ready, 1)
            for g in range(GROUPS):
                fill = sorted_in[g].rearrange("(n p k) d -> n p (k d)", p=P, n=FILLS)
                for n in range(FILLS):
                    sp.dma_start(fill[n], zeros[:]).then_inc(padded[g], 16)
            for g in range(GROUPS):
                spare = sorted_out[g][MIN_TILES * ST:MAX_TILES * ST, :].rearrange("(p k) d -> p (k d)", p=P)
                for n in range(SPARES):
                    w = spare.shape[1] // SPARES
                    sp.dma_start(spare[:, n * w:(n + 1) * w], zeros[:, 0:w]).then_inc(spares_filled, 16)

            def expert_io(f, g):
                k = (f, g)
                tiles_in = sorted_in[g].rearrange("(n p k) d -> n p k d", p=P, k=HALVES)
                tiles_out = sorted_out[g].rearrange("(n p k) d -> n p k d", p=P, k=HALVES)
                sp.wait_ge(scattered[k], 16 * TG)
                bounds = [sp.value_load(starts[g][0:1, E:E + 1], min_val=E, max_val=MAX_TILES)]
                total = bounds[0]
                sp.dma_start(x_in[:], tiles_in[0]).then_inc(x_in_loaded[k], 16)
                sp.wait_ge(xT_done[k], 1)
                sp.dma_start(x_in[:], tiles_in[1]).then_inc(x_in_loaded[k], 16)
                sp.wait_ge(spares_filled, 16 * GROUPS * SPARES)
                sp.sem_inc(y_stored[k], 16)
                with sp.Fori(0, total) as i:
                    sp.wait_ge(xT_done[k], i + 2)
                    sp.dma_start(x_in[:], tiles_in[bass.ds(i + 2, 1)]).then_inc(x_in_loaded[k], 16)
                    sp.wait_ge(y_copied[k], HALVES * i + 2 * HALVES)
                    sp.dma_start(tiles_out[bass.ds(i, 1)], y_sb[:]).then_inc(y_stored[k], 16)
                sp.wait_ge(x_in_loaded[k], 16 * (total + 2))
                sp.wait_ge(y_stored[k], 16 * (total + 1))
                sp.sem_inc(experts_done, 1)

            for f, g in phases:
                expert_io(f, g)
            for c in range(CHUNKS):
                sp.wait_ge(x_final, c + 1)
                sp.dma_start(out_chunks[:, c, :], x_sb[:, c, :]).then_inc(out_stored, 16)
            sp.wait_ge(out_stored, 16 * CHUNKS)

        @block.gpsimd
        def _(pool):
            pool.memset(zeros[:], 0.0).then_inc(zeros_ready, 1)
            pool.dma_start(gate_sb[:], gate_w).then_inc(weights_loaded, 16)
            pool.dma_start(gate_b_sb[:], gate_b.partition_broadcast(P)).then_inc(weights_loaded, 16)
            pool.dma_start(wqkv_sb[:], w_qkv).then_inc(weights_loaded, 16)
            pool.dma_start(bqkv_sb[:], b_qkv.partition_broadcast(P)).then_inc(weights_loaded, 16)

            def scatter(f, g):
                pool.wait_ge(routed, route_phase[f, g] + 1)
                if f == 0:
                    pool.wait_ge(padded[g], 16 * FILLS)
                for t in range(TG):
                    c = g * CPG + t // R
                    pool.indirect_dma_start(
                        out=sorted_in[g], out_offset=bass.IndirectOffsetOnAxis(ap=rows[g][:, t:t + 1], axis=0),
                        in_=xn_sb[:, c, t % R, :], in_offset=None).then_inc(scattered[f, g], 16)

            def gather(f, g):
                pool.wait_ge(spares_filled, 16 * GROUPS * SPARES)
                pool.wait_ge(experts_done, route_phase[f, g] + 1)
                for j in range(CPG):
                    n = route_phase[f, g] * CPG + j
                    if n >= 2:
                        pool.wait_ge(y_back_used, n - 1)
                    for r in range(R):
                        t = j * R + r
                        pool.indirect_dma_start(
                            out=y_back[:, n % 2, r * D:(r + 1) * D], out_offset=None, in_=sorted_out[g],
                            in_offset=bass.IndirectOffsetOnAxis(ap=rows[g][:, t:t + 1], axis=0),
                        ).then_inc(gathered[n % 2], 16)

            for f in range(2):
                for g in range(GROUPS):
                    scatter(f, g)
                for g in range(GROUPS):
                    gather(f, g)

        @block.scalar
        def _(act):
            act.dma_start(w1_sb[:], w1).then_inc(experts_loaded, 16)
            act.dma_start(w2_sb[:], w2).then_inc(experts_loaded, 16)
            act.dma_start(b1_sb[:], b1).then_inc(experts_loaded, 16)
            act.dma_start(b2_sb[:], b2.partition_broadcast(P)).then_inc(experts_loaded, 16)

            def deviation(step):
                act.wait_ge(var_ready, norm_phase[step] + 1)
                nc.scalar.activation(std[:], var[:], ACT.Sqrt).then_inc(std_ready, 1)

            def copy_xnT(step, j):
                n = norm_base[step] + j
                act.wait_ge(xnT_done, n + 1)
                nc.scalar.activation(xnT[:, n % 2, :, :], bank[0][:, :], ACT.Copy).then_inc(xnT_copied, 1)

            def experts(f, g):
                k = (f, g)
                act.wait_ge(experts_loaded, 64)
                act.wait_ge(routed, route_phase[k] + 1)
                bounds = expert_bounds(act, g)

                def copy_xT(i):
                    act.wait_ge(xT_done[k], i + 1)
                    nc.scalar.activation(xT[:], bank[6][:, 0:ST], ACT.Copy).then_inc(xT_copied[k], 1)

                copy_xT(0)
                for e in range(E):
                    with act.Fori(bounds[e], bounds[e + 1]) as i:
                        for c in range(1, HC, 2):
                            act.wait_ge(h_done[k], HC * i + c + 1)
                            nc.scalar.activation(hT[:, c, :], bank[c][:, 0:ST], ACT.Relu,
                                                 bias=b1_sb[:, e * HC + c:e * HC + c + 1]).then_inc(relu_a[k], 1)
                        copy_xT(i + 1)

            def attention(g):
                step = ("attn", 1, g)
                deviation(step)

                def split_q(j):
                    n = g * CPG + j
                    act.wait_ge(qT_done, n + 1)
                    for r in range(R):
                        s = slice(r * CLASS_CH, (r + 1) * CLASS_CH)
                        last = nc.scalar.activation(q_by_class[s, r, :], bank[2][s, 0:P], ACT.Copy)
                    last.then_inc(q_ready, 1)

                copy_xnT(step, 0)
                split_q(0)
                for j in range(CPG):
                    n = g * CPG + j
                    if j + 1 < CPG:
                        copy_xnT(step, j + 1)
                    for s in range(2):
                        act.wait_ge(shifted, 2 * n + s + 1)
                        part = probs[:, 2 * s:2 * s + 2, :]
                        nc.scalar.activation(part, part, ACT.Exp, scale=SCALE).then_inc(exp_done, 1)
                    for s in range(2):
                        act.wait_ge(probsT_done, 2 * n + s + 1)
                        nc.scalar.activation(probsT[:, 4 * s:4 * s + 4, :], bank[6 + s][:, :],
                                             ACT.Copy).then_inc(probsT_copied, 1)
                    if j + 1 < CPG:
                        split_q(j + 1)

            for kind, f, g in order[:GROUPS]:
                deviation((kind, f, g))
                for j in range(CPG):
                    copy_xnT((kind, f, g), j)
            for g in range(GROUPS):
                experts(0, g)
            act.wait_ge(consts_ready, 1)
            for kind, f, g in order[GROUPS:]:
                if kind == "attn":
                    attention(g)
                else:
                    deviation((kind, f, g))
                    for j in range(CPG):
                        copy_xnT((kind, f, g), j)
            for g in range(GROUPS):
                experts(1, g)

        @block.vector
        def _(dve):
            count = [0]

            def done(ins):
                count[0] += 1
                return ins.then_inc(v_done, 1)

            def own():
                dve.wait_ge(v_done, count[0])

            dve.wait_ge(consts_loaded, 16)
            done(nc.vector.tensor_copy(tri[:], cst[:, C_TRI:C_TRI + P]))
            done(nc.vector.memset(ones[:], 1.0))
            done(nc.vector.memset(q_by_class[:], 0.0))
            done(nc.vector.memset(v_pairs[:], 0.0))
            own()
            for h in range(2):
                s = slice(h * SEQ, (h + 1) * SEQ)
                at = h * (HEAD_DIM + 1) + HEAD_DIM
                for slot in range(2):
                    for b in range(2):
                        done(nc.vector.memset(v_pairs[s, slot, b, :, :, at:at + 1], 1.0))
            own()
            nc.vector.tensor_copy(probs[:, 0, 0:1], ones[:, 0:1]).then_inc(consts_ready, 1)
            dve.wait_ge(weights_loaded, 64)

            def moments(c, g):
                for r in range(R):
                    t = (c - g * CPG) * R + r
                    done(nc.vector.bn_stats(stats[:, t, :], x_sb[:, c, r * D:(r + 1) * D]))

            def normalise(step):
                g = step[2]
                own()
                me, mo = stats[:, :, 1], stats[:, :, 4]
                done(nc.vector.tensor_tensor(mean[:], me, mo, ALU.add))
                done(nc.vector.tensor_tensor(diff[:], me, mo, ALU.subtract))
                done(nc.vector.tensor_tensor(m2[:], stats[:, :, 2], stats[:, :, 5], ALU.add))
                own()
                done(nc.vector.tensor_scalar(mean[:], mean[:], 0.5, None, ALU.mult))
                done(nc.vector.tensor_tensor(diff[:], diff[:], diff[:], ALU.mult))
                done(nc.vector.tensor_scalar(m2[:], m2[:], 1.0 / D, EPS, ALU.mult, ALU.add))
                own()
                nc.vector.scalar_tensor_tensor(out=var[:], in0=diff[:], scalar=0.25, in1=m2[:],
                                               op0=ALU.mult, op1=ALU.add).then_inc(var_ready, 1)
                dve.wait_ge(std_ready, norm_phase[step] + 1)
                done(nc.vector.reciprocal(rstd[:], std[:]))
                own()
                for j in range(CPG):
                    c = g * CPG + j
                    for r in range(R):
                        t = j * R + r
                        last = nc.vector.tensor_scalar(xn_sb[:, c, r, :], x_sb[:, c, r * D:(r + 1) * D],
                                                       mean[:, t:t + 1], rstd[:, t:t + 1],
                                                       ALU.subtract, ALU.mult)
                    last.then_inc(xn_ready, 1)

            def route(f, g):
                k = route_phase[f, g]
                dve.wait_ge(logits_done, k + 1)
                iota = expert_iota.unsqueeze(1).to_broadcast([P, TG, E])
                done(nc.vector.tensor_tensor(logits[:], bank[2][:, 0:TG * E].rearrange("p (t e) -> p t e", e=E),
                                             gate_b_sb[:].unsqueeze(1).to_broadcast([P, TG, E]), ALU.add))
                own()
                done(nc.vector.tensor_reduce(top[:], logits[:], AX.X, ALU.max))
                own()
                done(nc.vector.tensor_tensor(hit[:], logits[:], top[:].unsqueeze(2).to_broadcast([P, TG, E]),
                                             ALU.is_ge))
                own()
                done(nc.vector.tensor_tensor(hit[:], hit[:], iota, ALU.mult))
                own()
                done(nc.vector.tensor_reduce(first[:], hit[:], AX.X, ALU.min))
                own()
                done(nc.vector.tensor_tensor(onehot[:], iota, first[:].unsqueeze(2).to_broadcast([P, TG, E]),
                                             ALU.is_equal))
                own()
                nc.vector.tensor_copy(hit[:], onehot[:]).then_inc(onehot_ready, 1)
                dve.wait_ge(ranks_done, k + 1)
                done(nc.vector.tensor_copy(scan[0][:].rearrange("p e t -> p t e"),
                                           bank[4][:, 0:TG * E].rearrange("p (t e) -> p t e", e=E)))
                own()
                src, shift = 0, 1
                while shift < TG:
                    a, b = scan[src], scan[1 - src]
                    done(nc.vector.tensor_tensor(b[:, :, shift:], a[:, :, shift:], a[:, :, :TG - shift], ALU.add))
                    done(nc.vector.tensor_copy(b[:, :, 0:shift], a[:, :, 0:shift]))
                    own()
                    src, shift = 1 - src, 2 * shift
                sums = scan[src]
                done(nc.vector.tensor_scalar(tiles_i[:], sums[:, :, TG - 1], float(ST - 1), None, ALU.add))
                own()
                done(nc.vector.tensor_scalar(tiles_i[:], tiles_i[:], ST.bit_length() - 1, None,
                                             ALU.arith_shift_right))
                own()
                done(nc.vector.tensor_scalar(tiles_f[:], tiles_i[:], 1.0, None, ALU.max))
                own()
                done(nc.vector.tensor_tensor(starts_m[:], lower, tiles_f[:].unsqueeze(1).to_broadcast([P, E + 1, E]),
                                             ALU.mult))
                own()
                done(nc.vector.tensor_reduce(starts_f[:], starts_m[:], AX.X, ALU.add))
                own()
                done(nc.vector.tensor_copy(starts[g][:], starts_f[:]))
                done(nc.vector.tensor_copy(place[:], bank[3][:, 0:TG * E].rearrange("p (t e) -> p t e", e=E)))
                own()
                done(nc.vector.tensor_tensor(place[:, 1:, :], place[:, 1:, :],
                                             sums[:, :, 0:TG - 1].rearrange("p e t -> p t e"), ALU.add))
                done(nc.vector.tensor_scalar(starts_f[:], starts_f[:], float(ST), None, ALU.mult))
                own()
                done(nc.vector.tensor_tensor(place[:], place[:],
                                             starts_f[:, 0:E].unsqueeze(1).to_broadcast([P, TG, E]), ALU.add))
                own()
                done(nc.vector.tensor_tensor(place[:], place[:], hit[:], ALU.mult))
                own()
                done(nc.vector.tensor_reduce(rows_f[:], place[:], AX.X, ALU.add))
                own()
                nc.vector.tensor_copy(rows[g][:], rows_f[:]).then_inc(routed, 1)

            def experts(f, g):
                k = (f, g)
                dve.wait_ge(experts_loaded, 64)
                dve.wait_ge(routed, route_phase[k] + 1)
                bounds = expert_bounds(dve, g)
                own()
                dve.sem_inc(y_copied[k], HALVES)
                for e in range(E):
                    with dve.Fori(bounds[e], bounds[e + 1]) as i:
                        for n, c in enumerate(range(0, HC, 2)):
                            dve.wait_ge(h_done[k], HC * i + c + 1)
                            nc.vector.tensor_scalar(hT[:, c, :], bank[c][:, 0:ST],
                                                    b1_sb[:, e * HC + c:e * HC + c + 1], 0.0,
                                                    ALU.add, ALU.max).then_inc(relu_v[k], 1)
                        dve.wait_ge(y_stored[k], 16 * (i + 1))
                        for h in range(HALVES):
                            dve.wait_ge(y_done[k], HALVES * i + h + 1)
                            nc.vector.tensor_tensor(y_sb[:, h, :], bank[4 + h][:, 0:D], b2_sb[:, e, :],
                                                    ALU.add).then_inc(y_copied[k], 1)

            def add_ffn(f, g, j):
                n = route_phase[f, g] * CPG + j
                c = g * CPG + j
                dve.wait_ge(gathered[n % 2], 16 * R * (n // 2 + 1))
                ins = nc.vector.scalar_tensor_tensor(out=x_sb[:, c, :], in0=y_back[:, n % 2, :], scalar=0.5,
                                                     in1=x_sb[:, c, :], op0=ALU.mult, op1=ALU.add)
                ins.then_inc(y_back_used, 1)
                return n

            def attention(g):
                def take_qkv(j):
                    n = g * CPG + j
                    dve.wait_ge(qkv_done, n + 1)
                    qkv = bank[1][:, 0:R * QKV].rearrange("p (r n) -> p r n", r=R)
                    nc.vector.tensor_tensor(qk[:].rearrange("p s r n -> p r s n"),
                                            qkv[:, :, 0:2 * CLASS_CH].rearrange("p r (s n) -> p r s n", s=2),
                                            bqkv_sb[:, :, 0:2 * CLASS_CH].rearrange("p r (s n) -> p r s n", s=2),
                                            ALU.add).then_inc(qk_ready, 1)
                    for b in range(2):
                        s = slice(b * SEQ, (b + 1) * SEQ)
                        for h in range(2):
                            at = h * (HEAD_DIM + 1)

                            def pair(ap):
                                return ap[s, :, 2 * CLASS_CH:].rearrange("p r (w h d) -> p r w h d", h=2,
                                                                         d=HEAD_DIM)[:, :, :, h, :]

                            last = nc.vector.tensor_tensor(
                                v_pairs[h * SEQ:(h + 1) * SEQ, n % 2, b, :, :, at:at + HEAD_DIM],
                                pair(qkv), pair(bqkv_sb), ALU.add)
                    last.then_inc(v_ready, 1)

                def split_k(j):
                    n = g * CPG + j
                    dve.wait_ge(kT_done, n + 1)
                    nc.vector.tensor_tensor(k_by_head[:], bank[3][:, 0:P].unsqueeze(1).to_broadcast([P, CLASS_HEADS, P]),
                                            head_mask.unsqueeze(2).to_broadcast([P, CLASS_HEADS, P]),
                                            ALU.mult).then_inc(k_ready, 1)

                take_qkv(0)
                split_k(0)
                for j in range(CPG):
                    n = g * CPG + j
                    for s in range(2):
                        dve.wait_ge(scores_done, 2 * n + s + 1)
                        sc = bank[4 + s][:, :].rearrange("p (h q) -> p h q", q=SEQ)
                        m = row_max[:, 8 * s:8 * s + 8]
                        done(nc.vector.tensor_reduce(m, sc, AX.X, ALU.max))
                        own()
                        nc.vector.tensor_tensor(
                            probs[:, 2 * s:2 * s + 2, :].rearrange("p r (h q) -> p (r h) q", q=SEQ), sc,
                            m.unsqueeze(2).to_broadcast([P, 8, SEQ]), ALU.subtract).then_inc(shifted, 1)
                    if j + 1 < CPG:
                        take_qkv(j + 1)
                        split_k(j + 1)
                    dve.wait_ge(ctx_done, n + 1)
                    got = bank[0][:, 0:R * CLASS_HEADS * (HEAD_DIM + 1)].rearrange("p (h d) -> p h d", d=HEAD_DIM + 1)
                    done(nc.vector.reciprocal(inv_sum[:], got[:, :, HEAD_DIM]))
                    own()
                    last = nc.vector.tensor_tensor(attended[:], got[:, :, 0:HEAD_DIM],
                                                   inv_sum[:].unsqueeze(2).to_broadcast([P, R * CLASS_HEADS, HEAD_DIM]),
                                                   ALU.mult)
                    last.then_inc(ctx_used, 1)
                    dve.wait_ge(ctx_used, n + 1)
                    c = g * CPG + j
                    for r in range(R):
                        at = x_sb[:, c, r * D:(r + 1) * D].rearrange("p (h s d) -> p h s d", s=R, d=HEAD_DIM)[:, :, r, :]
                        ins = nc.vector.tensor_tensor(at, at, attended[:, r * CLASS_HEADS:(r + 1) * CLASS_HEADS, :],
                                                      ALU.add)
                        done(ins)
                    own()
                    moments(c, g)

            for kind, f, g in order[:GROUPS]:
                for j in range(CPG):
                    c = g * CPG + j
                    dve.wait_ge(x_loaded[c * XL // CHUNKS], 16)
                    moments(c, g)
                normalise((kind, f, g))
                route(f, g)
            for g in range(GROUPS):
                experts(0, g)
            for g in range(GROUPS):
                for j in range(CPG):
                    n = add_ffn(0, g, j)
                    dve.wait_ge(y_back_used, n + 1)
                    moments(g * CPG + j, g)
                normalise(("attn", 1, g))
                attention(g)
                normalise(("ffn", 1, g))
                route(1, g)
            for g in range(GROUPS):
                experts(1, g)
            for g in range(GROUPS):
                for j in range(CPG):
                    n = add_ffn(1, g, j)
                    dve.wait_ge(y_back_used, n + 1)
                    nc.vector.tensor_copy(top[:, 0:1], top[:, 1:2]).then_inc(x_final, 1)

        @block.tensor
        def _(pe):
            def transpose_xn(step, j):
                n = norm_base[step] + j
                c = step[2] * CPG + j
                pe.wait_ge(xn_ready, n + 1)
                if n >= 1:
                    pe.wait_ge(xnT_copied, n)
                for r in range(R):
                    last = nc.tensor.transpose(bank[0][:, r * P:(r + 1) * P], xn_sb[:, c, r, :], ident)
                last.then_inc(xnT_done, 1)

            def gate(f, g):
                step = ("ffn", f, g)
                for j in range(CPG + 1):
                    if j < CPG:
                        transpose_xn(step, j)
                    if j >= 1:
                        n = norm_base[step] + j - 1
                        pe.wait_ge(xnT_copied, n + 1)
                        for r in range(R):
                            t = (j - 1) * R + r
                            last = nc.tensor.matmul(bank[2][:, t * E:(t + 1) * E], xnT[:, n % 2, r, :], gate_sb[:],
                                                    start=True, stop=True)
                last.then_inc(logits_done, 1)
                pe.wait_ge(onehot_ready, route_phase[f, g] + 1)
                flat = onehot[:].rearrange("p t e -> p (t e)")
                nc.tensor.matmul(bank[3][:, 0:TG * E], tri[:], flat, start=True, stop=True)
                nc.tensor.matmul(bank[4][:, 0:TG * E], ones[:], flat, start=True, stop=True).then_inc(ranks_done, 1)

            def experts(f, g):
                k = (f, g)
                pe.wait_ge(experts_loaded, 64)
                pe.wait_ge(routed, (f + 1) * GROUPS)
                bounds = expert_bounds(pe, g)

                def transpose_x(i):
                    pe.wait_ge(x_in_loaded[k], 16 * (i + 1))
                    for h in range(HALVES):
                        last = nc.tensor.transpose(bank[6][:, h * P:(h + 1) * P], x_in[:, h, :], ident)
                    last.then_inc(xT_done[k], 1)

                transpose_x(0)
                for e in range(E):
                    with pe.Fori(bounds[e], bounds[e + 1]) as i:
                        pe.wait_ge(xT_copied[k], i + 1)
                        for c in range(HC):
                            nc.tensor.matmul(bank[c][:, 0:ST], w1_sb[:, e, c * P:(c + 1) * P], xT[:],
                                             start=True, stop=True).then_inc(h_done[k], 1)
                        transpose_x(i + 1)
                        for h in range(HALVES):
                            pe.wait_ge(y_copied[k], HALVES * i + h + 1)
                            for c in range(HC):
                                if h == 0:
                                    pe.wait_ge(relu_a[k] if c % 2 else relu_v[k], HC // 2 * i + c // 2 + 1)
                                last = nc.tensor.matmul(bank[4 + h][:, 0:D], hT[:, c, h * P:(h + 1) * P],
                                                        w2_sb[:, e, c, :], start=(c == 0), stop=(c == HC - 1))
                            last.then_inc(y_done[k], 1)
                pe.wait_ge(xT_copied[k], bounds[E] + 1)
                pe.sem_inc(pe_phases, 1)

            def attention(g):
                step = ("attn", 1, g)

                def project(j):
                    n = norm_base[step] + j
                    m = g * CPG + j
                    pe.wait_ge(xnT_copied, n + 1)
                    if m >= 1:
                        pe.wait_ge(v_ready, m)
                    for r in range(R):
                        last = nc.tensor.matmul(bank[1][:, r * QKV:(r + 1) * QKV], xnT[:, n % 2, r, :],
                                                wqkv_sb[:, r, :], start=True, stop=True)
                    last.then_inc(qkv_done, 1)

                def transpose_qk(j):
                    pe.wait_ge(qk_ready, g * CPG + j + 1)
                    for s, done in ((0, qT_done), (1, kT_done)):
                        nc.tensor.transpose(bank[2 + s][:, 0:P], qk[:, s, :, :].rearrange("p r n -> p (r n)"),
                                            ident).then_inc(done, 1)

                transpose_xn(step, 0)
                project(0)
                transpose_qk(0)
                for j in range(CPG):
                    n = g * CPG + j
                    pe.wait_ge(q_ready, n + 1)
                    pe.wait_ge(k_ready, n + 1)
                    for r in range(R):
                        for b in range(2):
                            s = slice(b * SEQ, (b + 1) * SEQ)
                            last = nc.tensor.matmul(bank[4 + r // 2][s, (r % 2) * 256:(r % 2) * 256 + 256],
                                                    q_by_class[:, r, s], k_by_head[:, :, s], start=True, stop=True)
                        if r % 2:
                            last.then_inc(scores_done, 1)
                    if j + 1 < CPG:
                        if n >= 1:
                            pe.wait_ge(ctx_used, n)
                        transpose_xn(step, j + 1)
                        project(j + 1)
                    for s in range(2):
                        pe.wait_ge(exp_done, 2 * n + s + 1)
                        for u in range(4):
                            r, w = 2 * s + u // 2, u % 2
                            last = nc.tensor.transpose(bank[6 + s][:, u * P:(u + 1) * P],
                                                       probs[:, r, w * P:(w + 1) * P], ident)
                        last.then_inc(probsT_done, 1)
                    if j + 1 < CPG:
                        transpose_qk(j + 1)
                    pe.wait_ge(v_ready, n + 1)
                    for s in range(2):
                        pe.wait_ge(probsT_copied, 2 * n + s + 1)
                        for u in range(4):
                            r, w = 2 * s + u // 2, u % 2
                            at = (r * ROWS + w) * 2 * (HEAD_DIM + 1)
                            for b in range(2):
                                q = slice(b * SEQ, (b + 1) * SEQ)
                                last = nc.tensor.matmul(bank[0][q, at:at + 2 * (HEAD_DIM + 1)],
                                                        probsT[:, r * ROWS + w, q], v_pairs[:, n % 2, b, r, w, :],
                                                        start=True, stop=True)
                    last.then_inc(ctx_done, 1)
                pe.wait_ge(ctx_used, (g + 1) * CPG)

            pe.wait_ge(consts_loaded, 16)
            pe.wait_ge(weights_loaded, 64)
            for g in range(GROUPS):
                gate(0, g)
            for g in range(GROUPS):
                experts(0, g)
            pe.wait_ge(consts_ready, 1)
            for g in range(GROUPS):
                attention(g)
                gate(1, g)
            for g in range(GROUPS):
                experts(1, g)


def kernel(L0_attn_X, L0_attn_Wq, L0_attn_bq, L0_attn_Wkv, L0_attn_bkv, L0_ffn_gate_w, L0_ffn_gate_b,
           L0_ffn_w1, L0_ffn_b1, L0_ffn_w2, L0_ffn_b2):
    import concourse.bacc as bacc
    from concourse.bass_utils import run_bass_kernel_spmd

    shape = np.shape(L0_attn_X)
    d = shape[-1]
    e, hid, _ = np.shape(L0_ffn_w1)

    def by_class(w, parts):
        w = np.asarray(w).reshape(-1, parts, CLASS_HEADS, R, HEAD_DIM)
        return w.transpose(0, 3, 1, 2, 4).reshape(-1, R, parts * CLASS_CH)

    arrays = {
        "x": np.asarray(L0_attn_X).reshape(-1, d),
        "w_qkv": np.concatenate([by_class(L0_attn_Wq, 1), by_class(L0_attn_Wkv, 2)], axis=2),
        "b_qkv": np.concatenate([by_class(L0_attn_bq, 1), by_class(L0_attn_bkv, 2)], axis=2)[0],
        "gate_w": np.asarray(L0_ffn_gate_w).T,
        "gate_b": np.asarray(L0_ffn_gate_b),
        "w1": np.asarray(L0_ffn_w1).transpose(2, 0, 1),
        "b1": np.asarray(L0_ffn_b1).reshape(e * hid // P, P).T,
        "w2": np.asarray(L0_ffn_w2).reshape(e, d, hid // P, P).transpose(3, 0, 2, 1),
        "b2": np.asarray(L0_ffn_b2),
        "consts": shape_constants(e),
    }
    nc = bacc.Bacc("TRN2", target_bir_lowering=False, num_devices=1)
    maps, args = {}, []
    for name, a in arrays.items():
        a = np.ascontiguousarray(a)
        maps[f"in_{name}"] = a
        args.append(nc.dram_tensor(f"in_{name}", a.shape, mybir.dt.from_np(a.dtype), kind="ExternalInput").ap())
    args.append(nc.dram_tensor("out_x", arrays["x"].shape, F32, kind="ExternalOutput").ap())
    macaron_kernel(nc, *args)
    got = run_bass_kernel_spmd(nc, [maps], core_ids=[0])
    return got.results[0]["out_x"].reshape(shape)
```

```python
from contextlib import ExitStack

import numpy as np

import concourse.bass as bass
from concourse import mybir

ALU = mybir.AluOpType
ACT = mybir.ActivationFunctionType
AX = mybir.AxisListType
F32 = mybir.dt.float32
BF16 = mybir.dt.bfloat16
I32 = mybir.dt.int32
U32 = mybir.dt.uint32

P = 128
HEADS, HEAD_DIM, R = 16, 8, 4
CLASS_HEADS = HEADS // R
CLASS_CH = CLASS_HEADS * HEAD_DIM
ROWS = CLASS_HEADS // 2
PAIR = 2 * (HEAD_DIM + 1)

C_IDENT, C_TRI, C_IOTA, C_LOWER, C_HEAD, C_END = 0, 128, 256, 264, 336, 340


def shape_constants(experts):
    c = np.zeros((P, C_END), np.float32)
    k = np.arange(P)
    c[:, C_IDENT:C_IDENT + P] = k[:, None] == k[None, :]
    c[:, C_TRI:C_TRI + P] = k[:, None] < k[None, :]
    e = np.arange(experts)
    c[:, C_IOTA:C_IOTA + experts] = e - experts
    c[:, C_LOWER:C_LOWER + (experts + 1) * experts] = (e[None, :] < np.arange(experts + 1)[:, None]).reshape(1, -1)
    c[:, C_HEAD:C_HEAD + CLASS_HEADS] = (k[:, None] % CLASS_CH) // HEAD_DIM == np.arange(CLASS_HEADS)[None, :]
    return c


def macaron_kernel(nc, x, w_qkv, b_qkv, gate_w, gate_b, w1, b1, w2, b2, consts, out):
    TOKENS, D = x.shape
    E = gate_w.shape[1]
    HID = w1.shape[2]
    HC = HID // P
    CHUNKS = TOKENS // (P * R)
    HEAD = CHUNKS * 3 // 8
    TAIL = CHUNKS * 3 // 8
    MAIN = CHUNKS - TAIL
    groups = {(0, 0): (0, HEAD, 0), (0, 1): (HEAD, CHUNKS - HEAD, 1), (1, 0): (0, MAIN, 1), (1, 1): (MAIN, TAIL, 0)}
    phases = list(groups)
    norms = {("ffn0", 0): HEAD, ("ffn0", HEAD): CHUNKS - HEAD, ("attn", 0): HEAD, ("attn", HEAD): MAIN - HEAD,
             ("ffn1", 0): HEAD, ("attn", MAIN): TAIL, ("ffn1", HEAD): MAIN - HEAD,
             ("ffn1", MAIN): TAIL // 2, ("ffn1", MAIN + TAIL // 2): TAIL - TAIL // 2}
    TG_MAX = max(chunks for _, chunks, _ in groups.values()) * R
    QUAD = 4
    SEQ = P // 2
    AHEAD = 2
    QUARTER = P // R
    LOGIT_BANKS, RANK_BANK = (4, 6, 3), 7
    GATE_BANKS = 2
    sizes = [[chunks * R for _, chunks, buffer in groups.values() if buffer == b] for b in range(2)]
    MIN_TILES = [min(n) for n in sizes]
    MAX_TILES = [max(n) + E for n in sizes]
    LOADED_TILES = [-(-(n + AHEAD) // QUAD) * QUAD for n in MAX_TILES]
    ROWS_CAP = [n * P for n in LOADED_TILES]
    EPS = 1e-5
    FILLS, SPARES = 4, 2
    FILL = [n * D // P // FILLS for n in ROWS_CAP]
    SCALE = float(1.0 / np.sqrt(HEAD_DIM))
    QKV = 3 * CLASS_CH

    sorted_in = [nc.dram_tensor(f"sorted_in{b}", (ROWS_CAP[b], D), F32, kind="Internal").ap() for b in range(2)]
    sorted_out = [nc.dram_tensor(f"sorted_out{b}", (MAX_TILES[b] * P, D), F32, kind="Internal").ap() for b in range(2)]
    x_chunks = x.rearrange("(c p r) d -> p c (r d)", p=P, r=R)
    out_chunks = out.rearrange("(c p r) d -> p c (r d)", p=P, r=R)

    with ExitStack() as ctx:
        def sb(name, shape, dt=F32):
            return ctx.enter_context(nc.sbuf_tensor(name, shape, dt))

        def sem(name):
            return ctx.enter_context(nc.semaphore(name))

        bank = [ctx.enter_context(nc.psum_tensor(f"bank{i}", [P, 512], F32)) for i in range(8)]

        cst = sb("cst", [P, C_END])
        ident = cst[:, C_IDENT:C_IDENT + P]
        expert_iota = cst[:, C_IOTA:C_IOTA + E]
        lower = cst[:, C_LOWER:C_LOWER + (E + 1) * E].rearrange("p (i e) -> p i e", e=E)
        head_mask = cst[:, C_HEAD:C_HEAD + CLASS_HEADS]
        tri = sb("tri", [P, P], BF16)
        ones = sb("ones", [P, P], BF16)
        w1_sb = sb("w1_sb", [P, E, HID])
        w2_sb = sb("w2_sb", [P, E, HC, D])
        b1_sb = sb("b1_sb", [P, E * HC])
        b2_sb = sb("b2_sb", [P, E, D])
        gate_sb = sb("gate_sb", [P, QUARTER])
        gate_b_sb = sb("gate_b_sb", [P, E])
        wqkv_sb = sb("wqkv_sb", [P, R, QKV])
        bqkv_sb = sb("bqkv_sb", [P, R, QKV])
        x_sb = sb("x_sb", [P, CHUNKS, R * D])
        xn_sb = sb("xn_sb", [P, CHUNKS, R, D])
        kinds = {"attn": "attn", "ffn0": "ffn", "ffn1": "ffn"}
        by_use = {name: {kind: sb(f"{name}_{kind}", shape) for kind in ("attn", "ffn")} for name, shape in
                  (("stats", [P, CHUNKS * R, 6]), ("mean", [P, CHUNKS * R]), ("rstd", [P, CHUNKS * R]),
                   ("offset", [P, CHUNKS * R]))}
        stats, mean, rstd, offset = ({use: by_use[name][kind] for use, kind in kinds.items()}
                                     for name in ("stats", "mean", "rstd", "offset"))
        var = sb("var", [P, TG_MAX])
        diff = sb("diff", [P, TG_MAX])
        m2 = sb("m2", [P, TG_MAX])
        std = sb("std", [P, TG_MAX])
        xnT = sb("xnT", [P, 2, R, P])
        logitsT = sb("logitsT", [P, 2, P])
        logits = sb("logits", [P, TG_MAX, E])
        top = sb("top", [P, TG_MAX])
        hit = sb("hit", [P, TG_MAX, E])
        first = sb("first", [P, TG_MAX])
        onehot = sb("onehot", [P, TG_MAX, E], BF16)
        place = sb("place", [P, TG_MAX, E])
        tiles_i = sb("tiles_i", [P, E], I32)
        starts_m = sb("starts_m", [P, E + 1, E])
        starts_f = sb("starts_f", [P, E + 1])
        starts = {k: sb(f"starts_{k[0]}{k[1]}", [P, E + 1], I32) for k in phases}
        rows_f = sb("rows_f", [P, TG_MAX])
        rows = {k: sb(f"rows_{k[0]}{k[1]}", [P, groups[k][1] * R], U32) for k in phases}
        zeros = sb("zeros", [P, max(FILL)])
        tiles = [sb(f"tiles{b}", [P, LOADED_TILES[b], D]) for b in range(2)]
        x_stage = sb("x_stage", [P, D])
        xT = sb("xT", [P, P])
        hT = sb("hT", [P, HC, P])
        V_SLOTS = 3
        qk = sb("qk", [P, 2, R, CLASS_CH])
        q_by_class = sb("q_by_class", [P, R, P])
        k_by_head = sb("k_by_head", [P, CLASS_HEADS, P])
        v_pairs = sb("v_pairs", [P, V_SLOTS, R, ROWS, 2, PAIR])
        row_max = sb("row_max", [P, R * CLASS_HEADS])
        probs = sb("probs", [P, 2, R, CLASS_HEADS * SEQ])
        probsT = sb("probsT", [P, R * ROWS, P])
        inv_sum = sb("inv_sum", [P, R * CLASS_HEADS])
        attended = sb("attended", [P, R * CLASS_HEADS, HEAD_DIM])

        consts_loaded, weights_loaded = sem("consts_loaded"), sem("weights_loaded")
        XL = 8
        x_loaded = [sem(f"x_loaded{i}") for i in range(XL)]
        experts_loaded, halved = sem("experts_loaded"), sem("halved")
        gate_cleared = sem("gate_cleared")
        zeros_ready = sem("zeros_ready")
        padded = [sem(f"padded{b}") for b in range(2)]
        spares_filled = sem("spares_filled")
        v_done = sem("v_done")
        consts_ready = sem("consts_ready")
        var_ready, std_ready = sem("var_ready"), sem("std_ready")
        rstd_ready = sem("rstd_ready")
        xn_ready = [sem(f"xn_ready{c}") for c in range(CHUNKS)]
        xnT_done, xnT_copied = sem("xnT_done"), sem("xnT_copied")
        logitsT_done, logitsT_copied = sem("logitsT_done"), sem("logitsT_copied")
        logits_done, onehot_ready, ranks_done = sem("logits_done"), sem("onehot_ready"), sem("ranks_done")
        routed = sem("routed")
        scattered = {k: sem(f"scattered_{k[0]}{k[1]}") for k in phases}
        tiles_loaded = {k: sem(f"tiles_loaded_{k[0]}{k[1]}") for k in phases}
        x_staged = {k: sem(f"x_staged_{k[0]}{k[1]}") for k in phases}
        xT_done = {k: sem(f"xT_done_{k[0]}{k[1]}") for k in phases}
        xT_copied = {k: sem(f"xT_copied_{k[0]}{k[1]}") for k in phases}
        h_done = {k: sem(f"h_done_{k[0]}{k[1]}") for k in phases}
        relu_v = {k: sem(f"relu_v_{k[0]}{k[1]}") for k in phases}
        relu_a = {k: sem(f"relu_a_{k[0]}{k[1]}") for k in phases}
        y_done = {k: sem(f"y_done_{k[0]}{k[1]}") for k in phases}
        y_copied = {k: sem(f"y_copied_{k[0]}{k[1]}") for k in phases}
        y_stored = {k: sem(f"y_stored_{k[0]}{k[1]}") for k in phases}
        experts_done, pe_phases, v_phases = sem("experts_done"), sem("pe_phases"), sem("v_phases")
        gathered = [sem(f"gathered{c}") for c in range(CHUNKS)]
        ffn_added = [sem(f"ffn_added{c}") for c in range(CHUNKS)]
        qkv_done, qk_ready, v_ready = sem("qkv_done"), sem("qk_ready"), sem("v_ready")
        qT_done, q_ready, kT_done, k_ready = sem("qT_done"), sem("q_ready"), sem("kT_done"), sem("k_ready")
        scores_done, shifted, exp_done = sem("scores_done"), sem("shifted"), sem("exp_done")
        probsT_done, probsT_copied = sem("probsT_done"), sem("probsT_copied")
        ctx_done, ctx_used = sem("ctx_done"), sem("ctx_used")
        out_stored = sem("out_stored")

        block = ctx.enter_context(nc.Block())

        norm_phase = {step: i for i, step in enumerate(norms)}
        transposed = [("ffn0", 0, CHUNKS), ("attn", 0, MAIN), ("ffn1", 0, MAIN), ("attn", MAIN, TAIL),
                      ("ffn1", MAIN, TAIL)]
        norm_at = {step: i for i, step in enumerate(
            (use, at + j) for use, at, chunks in transposed for j in range(chunks))}
        batch_of = {(use, at + j): (use, at) for (use, at), chunks in norms.items() for j in range(chunks)}
        norm_round = {"ffn0": 1, "attn": 2, "ffn1": 3}
        deviations = {0: {HEAD - 4: [("attn", HEAD)], HEAD + 1: [("ffn1", 0)], MAIN - 1: [("attn", MAIN)]},
                      MAIN: {TAIL // 2 + 1: [("ffn1", MAIN)]}}
        scaled_at_end = {0: {MAIN - 2: [("ffn1", c) for c in range(2)],
                             MAIN - 1: [("ffn1", c) for c in range(2, HEAD - 1)]},
                         MAIN: {TAIL - 1: [("ffn1", MAIN + c) for c in range(TAIL // 2)]}}
        late_moments = {0: {}, MAIN: {}}
        for c in range(HEAD, MAIN):
            late_moments[0].setdefault(max(0, HEAD - 5 - (MAIN - 1 - c) // 2), []).append(c)
        for c in range(MAIN, CHUNKS):
            late_moments[0].setdefault(HEAD - 3 + c - MAIN, []).append(c)
        FIRST_MOMENTS, FIRST_NORM = E // 4, E - 3

        EARLY = (CHUNKS - HEAD) // 2

        def score_batches(k):
            tg = groups[k][1] * R
            return [slice(i, min(tg, i + 4 * R)) for i in range(0, tg, 4 * R)]

        onehot_base = {k: sum(len(score_batches(p)) for p in phases[:i]) for i, k in enumerate(phases)}
        logits_base = {k: sum(groups[p][1] for p in phases[:i]) for i, k in enumerate(phases)}
        route_phase = {k: i for i, k in enumerate(phases)}
        attention_runs = [(0, MAIN), (MAIN, TAIL)]

        def end_of(eng, k, e):
            eng.wait_ge(routed, route_phase[k] + 1)
            return eng.value_load(starts[k][0:1, e + 1:e + 2], min_val=e + 1, max_val=MAX_TILES[groups[k][2]])

        def expert_bounds(eng, k):
            return [0] + [end_of(eng, k, e) for e in range(E)]

        def expert_total(eng, k):
            return eng.value_load(starts[k][0:1, E:E + 1], min_val=E, max_val=MAX_TILES[groups[k][2]])

        def load_tiles(eng, k):
            _, chunks, b = groups[k]
            quads_in = sorted_in[b].rearrange("(m q p) d -> m p q d", p=P, q=QUAD)
            eng.wait_ge(scattered[k], 16 * chunks * R)
            total = expert_total(eng, k)
            eng.dma_start(tiles[b][:, 0:QUAD, :], quads_in[0]).then_inc(tiles_loaded[k], 16)
            with eng.Fori(1, (total + (AHEAD + QUAD - 1)) // QUAD) as m:
                eng.wait_ge(tiles_loaded[k], 16 * m)
                eng.dma_start(tiles[b][:, bass.ds(QUAD * m, QUAD), :],
                             quads_in[bass.ds(m, 1)]).then_inc(tiles_loaded[k], 16)

        def add_ffn(eng, f, c):
            eng.wait_ge(gathered[c], 16 * R * (f + 1))
            eng.tensor_tensor(x_sb[:, c, :], x_sb[:, c, :], xn_sb[:, c, :, :].rearrange("p r d -> p (r d)"),
                              ALU.add).then_inc(ffn_added[c], 1)

        def scale(eng, use, c):
            for r in range(R):
                i = c * R + r
                last = eng.tensor_scalar(xn_sb[:, c, r, :], x_sb[:, c, r * D:(r + 1) * D], mean[use][:, i:i + 1],
                                         rstd[use][:, i:i + 1], ALU.subtract, ALU.mult)
            last.then_inc(xn_ready[c], 1)

        @block.sync
        def _(sp):
            per = CHUNKS // XL
            for i in range(XL):
                sp.dma_start(x_sb[:, i * per:(i + 1) * per, :],
                             x_chunks[:, i * per:(i + 1) * per, :]).then_inc(x_loaded[i], 16)

            def pad(b):
                fill = sorted_in[b].rearrange("(n p k) d -> n p (k d)", p=P, n=FILLS)
                for n in range(FILLS):
                    sp.dma_start(fill[n], zeros[:, 0:FILL[b]]).then_inc(padded[b], 16)

            sp.wait_ge(zeros_ready, 1)
            pad(0)
            sp.dma_start(w1_sb[:], w1).then_inc(experts_loaded, 16)
            sp.dma_start(b1_sb[:], b1).then_inc(experts_loaded, 16)
            sp.dma_start(w2_sb[:], w2).then_inc(experts_loaded, 16)
            sp.dma_start(b2_sb[:], b2.partition_broadcast(P)).then_inc(experts_loaded, 16)
            pad(1)
            for b in range(2):
                spare = sorted_out[b][MIN_TILES[b] * P:MAX_TILES[b] * P, :].rearrange("(p k) d -> p (k d)", p=P)
                for n in range(SPARES):
                    w = spare.shape[1] // SPARES
                    sp.dma_start(spare[:, n * w:(n + 1) * w], zeros[:, 0:w]).then_inc(spares_filled, 16)

            def store_tiles(k):
                b = groups[k][2]
                tiles_out = sorted_out[b].rearrange("(n p) d -> n p d", p=P)
                with sp.Fori(0, expert_total(sp, k)) as i:
                    sp.wait_ge(y_copied[k], i + 2)
                    sp.dma_start(tiles_out[bass.ds(i, 1)], tiles[b][:, bass.ds(i, 1), :]).then_inc(y_stored[k], 16)

            sp.wait_ge(spares_filled, 16 * 2 * SPARES)
            for f in range(2):
                load_tiles(sp, (f, 0))
                for g in range(2):
                    store_tiles((f, g))
            for c in range(CHUNKS):
                sp.wait_ge(ffn_added[c], 2)
                sp.dma_start(out_chunks[:, c, :], x_sb[:, c, :]).then_inc(out_stored, 16)
            sp.wait_ge(out_stored, 16 * CHUNKS)

        @block.gpsimd
        def _(pool):
            def scatter(k):
                at, chunks, b = groups[k]
                pool.wait_ge(routed, route_phase[k] + 1)
                pool.wait_ge(padded[b], 16 * FILLS)
                for t in range(chunks * R):
                    pool.indirect_dma_start(
                        out=sorted_in[b], out_offset=bass.IndirectOffsetOnAxis(ap=rows[k][:, t:t + 1], axis=0),
                        in_=xn_sb[:, at + t // R, t % R, :], in_offset=None).then_inc(scattered[k], 16)

            def gather(k):
                at, chunks, b = groups[k]
                pool.wait_ge(spares_filled, 16 * 2 * SPARES)
                pool.wait_ge(y_stored[k], 16 * expert_total(pool, k))
                pool.sem_inc(experts_done, 1)
                for j in range(chunks + 1):
                    if j < chunks:
                        for r in range(R):
                            t = j * R + r
                            pool.indirect_dma_start(
                                out=xn_sb[:, at + j, r, :], out_offset=None, in_=sorted_out[b],
                                in_offset=bass.IndirectOffsetOnAxis(ap=rows[k][:, t:t + 1], axis=0),
                            ).then_inc(gathered[at + j], 16)
                    if j >= 1 and k != phases[-1]:
                        add_ffn(pool, k[0], at + j - 1)

            scatter((0, 0))
            scatter((0, 1))
            load_tiles(pool, (0, 1))
            gather((0, 0))
            gather((0, 1))
            scatter((1, 0))
            scatter((1, 1))
            load_tiles(pool, (1, 1))
            gather((1, 0))
            gather((1, 1))

        @block.scalar
        def _(act):
            act.dma_start(cst[:], consts).then_inc(consts_loaded, 16)
            act.dma_start(gate_b_sb[:], gate_b.partition_broadcast(P)).then_inc(weights_loaded, 16)
            act.dma_start(wqkv_sb[:], w_qkv).then_inc(weights_loaded, 16)
            act.dma_start(bqkv_sb[:], b_qkv.partition_broadcast(P)).then_inc(weights_loaded, 16)
            act.wait_ge(gate_cleared, 1)
            act.dma_start(gate_sb[:, 0:E], gate_w).then_inc(weights_loaded, 16)

            def deviation(step):
                act.wait_ge(var_ready, norm_phase[step] + 1)
                n = norms[step] * R
                nc.scalar.activation(std[:, 0:n], var[:, 0:n], ACT.Sqrt).then_inc(std_ready, 1)

            def scale_a(use, c):
                act.wait_ge(rstd_ready, norm_phase[batch_of[use, c]] + 1)
                for r in range(R):
                    i = c * R + r
                    last = nc.scalar.activation(xn_sb[:, c, r, :], x_sb[:, c, r * D:(r + 1) * D], ACT.Identity,
                                                bias=offset[use][:, i:i + 1], scale=rstd[use][:, i:i + 1])
                last.then_inc(xn_ready[c], 1)

            def copy_xnT(n, banks=1):
                act.wait_ge(xnT_done, n + 1)
                nc.scalar.activation(xnT[:, n % 2, :, :], bank[n % banks][:, :], ACT.Copy).then_inc(xnT_copied, 1)

            def experts(k, bounds, between=None):
                act.wait_ge(experts_loaded, 64)
                act.sem_inc(relu_a[k], HC // 2)

                def copy_xT(i):
                    act.wait_ge(xT_done[k], i + 1)
                    nc.scalar.activation(xT[:], bank[6][:, 0:P], ACT.Copy).then_inc(xT_copied[k], 1)

                copy_xT(0)
                for e in range(E):
                    with act.Fori(bounds[e], bounds[e + 1]) as i:
                        for c in range(0, HC // 2):
                            act.wait_ge(h_done[k], HC * i + c + 1)
                            nc.scalar.activation(hT[:, c, :], bank[c][:, 0:P], ACT.Relu,
                                                 bias=b1_sb[:, e * HC + c:e * HC + c + 1]).then_inc(relu_a[k], 1)
                        copy_xT(i + 1)
                    if between:
                        between(e)

            def attention(at, chunks):
                base = norm_at["attn", at]

                def split_q(j):
                    act.wait_ge(qT_done, at + j + 1)
                    for r in range(R):
                        s = slice(r * CLASS_CH, (r + 1) * CLASS_CH)
                        last = nc.scalar.activation(q_by_class[s, r, :], bank[2][s, 0:P], ACT.Copy)
                    last.then_inc(q_ready, 1)

                def split_k(j):
                    act.wait_ge(kT_done, at + j + 1)
                    for h in range(CLASS_HEADS):
                        last = nc.scalar.activation(k_by_head[:, h, :], bank[3][:, 0:P], ACT.Copy,
                                                    scale=head_mask[:, h:h + 1])
                    last.then_inc(k_ready, 1)

                def softmax_exp(j):
                    n = at + j
                    for s in range(2):
                        act.wait_ge(shifted, 2 * n + s + 1)
                        part = probs[:, n % 2, 2 * s:2 * s + 2, :]
                        nc.scalar.activation(part, part, ACT.Exp, scale=SCALE).then_inc(exp_done, 1)

                def copy_probsT(j):
                    n = at + j
                    for s in range(2):
                        act.wait_ge(probsT_done, 2 * n + s + 1)
                        nc.scalar.activation(probsT[:, 4 * s:4 * s + 4, :], bank[6 + s][:, :],
                                             ACT.Copy).then_inc(probsT_copied, 1)

                if at == 0:
                    scale_a("attn", 2)
                copy_xnT(base)
                copy_xnT(base + 1)
                for j in range(2):
                    split_q(j)
                    split_k(j)
                softmax_exp(0)
                for j in range(chunks):
                    if j + 2 < chunks:
                        copy_xnT(base + j + 2)
                    if batch_of["attn", at + min(j + 3, chunks - 1)] == ("attn", 0):
                        scale_a("attn", at + j + 3)
                    copy_probsT(j)
                    for step in deviations[at].get(j, ()):
                        deviation(step)
                    if j + 2 < chunks:
                        split_q(j + 2)
                        split_k(j + 2)
                    if j + 1 < chunks:
                        softmax_exp(j + 1)
                    for use, c in scaled_at_end[at].get(j, ()):
                        scale_a(use, c)

            def gate(k, inside=(), scaled=None):
                at, chunks, _ = groups[k]
                for j in range(chunks + 1):
                    if j == 1:
                        for step in inside:
                            deviation(step)
                    if j < chunks:
                        copy_xnT(norm_at[f"ffn{k[0]}", at + j], GATE_BANKS)
                    if j >= 1:
                        i = j - 1
                        act.wait_ge(logitsT_done, logits_base[k] + i + 1)
                        nc.scalar.activation(logitsT[:, i % 2, :], bank[(2, 5)[i % 2]][:, 0:P],
                                             ACT.Copy).then_inc(logitsT_copied, 1)
                    for use, c in (scaled or {}).get(j, ()):
                        scale_a(use, c)

            def first_attn(e):
                if e == FIRST_NORM:
                    deviation(("attn", 0))
                if e > FIRST_NORM:
                    scale_a("attn", e - FIRST_NORM - 1)

            deviation(("ffn0", 0))
            gate((0, 0))
            deviation(("ffn0", HEAD))
            gate((0, 1))
            act.wait_ge(experts_loaded, 64)
            nc.scalar.activation(w2_sb[:], w2_sb[:], ACT.Copy, scale=0.5).then_inc(halved, 1)
            nc.scalar.activation(b2_sb[:], b2_sb[:], ACT.Copy, scale=0.5).then_inc(halved, 1)
            next_bounds = [0]
            experts((0, 0), expert_bounds(act, (0, 0)), lambda e: next_bounds.append(end_of(act, (0, 1), e)))
            experts((0, 1), next_bounds, first_attn)
            act.wait_ge(consts_ready, 1)
            attention(*attention_runs[0])
            gate((1, 0), [("ffn1", HEAD)], {0: [("ffn1", HEAD - 1)]})
            attention(*attention_runs[1])
            gate((1, 1), [("ffn1", MAIN + TAIL // 2)])
            next_bounds = [0]
            experts((1, 0), expert_bounds(act, (1, 0)), lambda e: next_bounds.append(end_of(act, (1, 1), e)))
            experts((1, 1), next_bounds)

        @block.vector
        def _(dve):
            count = [0]

            def done(ins):
                count[0] += 1
                return ins.then_inc(v_done, 1)

            def own():
                dve.wait_ge(v_done, count[0])

            nc.vector.memset(gate_sb[:], 0.0).then_inc(gate_cleared, 1)
            nc.vector.memset(zeros[:], 0.0).then_inc(zeros_ready, 1)
            dve.wait_ge(consts_loaded, 16)
            done(nc.vector.tensor_copy(tri[:], cst[:, C_TRI:C_TRI + P]))
            done(nc.vector.memset(ones[:], 1.0))
            done(nc.vector.memset(q_by_class[:], 0.0))
            done(nc.vector.memset(v_pairs[:], 0.0))
            own()
            for h in range(2):
                s = slice(h * SEQ, (h + 1) * SEQ)
                at = h * (HEAD_DIM + 1) + HEAD_DIM
                for slot in range(V_SLOTS):
                    for r in range(R):
                        done(nc.vector.memset(v_pairs[s, slot, r, :, :, at:at + 1], 1.0))
            own()
            nc.vector.tensor_copy(probs[:, 0, 0, 0:1], ones[:, 0:1]).then_inc(consts_ready, 1)
            def moments(use, c):
                for r in range(R):
                    done(nc.vector.bn_stats(stats[use][:, c * R + r, :], x_sb[:, c, r * D:(r + 1) * D]))

            def variance(step):
                use, at = step
                n = norms[step] * R
                t = slice(at * R, at * R + n)
                own()
                mu = mean[use][:, t]
                me, mo = stats[use][:, t, 1], stats[use][:, t, 4]
                done(nc.vector.tensor_tensor(mu, me, mo, ALU.add))
                done(nc.vector.tensor_tensor(diff[:, 0:n], me, mo, ALU.subtract))
                done(nc.vector.tensor_tensor(m2[:, 0:n], stats[use][:, t, 2], stats[use][:, t, 5], ALU.add))
                own()
                done(nc.vector.tensor_scalar(mu, mu, 0.5, None, ALU.mult))
                done(nc.vector.tensor_tensor(diff[:, 0:n], diff[:, 0:n], diff[:, 0:n], ALU.mult))
                done(nc.vector.tensor_scalar(m2[:, 0:n], m2[:, 0:n], 1.0 / D, EPS, ALU.mult, ALU.add))
                own()
                if norm_phase[step]:
                    dve.wait_ge(std_ready, norm_phase[step])
                nc.vector.scalar_tensor_tensor(out=var[:, 0:n], in0=diff[:, 0:n], scalar=0.25, in1=m2[:, 0:n],
                                               op0=ALU.mult, op1=ALU.add).then_inc(var_ready, 1)

            def invert(step):
                use, at = step
                n = norms[step] * R
                dve.wait_ge(std_ready, norm_phase[step] + 1)
                t = slice(at * R, at * R + n)
                done(nc.vector.reciprocal(rstd[use][:, t], std[:, 0:n]))
                own()
                nc.vector.scalar_tensor_tensor(out=offset[use][:, t], in0=mean[use][:, t], scalar=-1.0,
                                               in1=rstd[use][:, t], op0=ALU.mult, op1=ALU.mult).then_inc(rstd_ready, 1)
                dve.wait_ge(rstd_ready, norm_phase[step] + 1)

            def normalise(step):
                variance(step)
                invert(step)
                for c in range(step[1], step[1] + norms[step]):
                    scale(dve, step[0], c)

            def per_expert(ap, w):
                return ap.unsqueeze(1).to_broadcast([P, w, E])

            def pick(k):
                def per_token(ap):
                    return ap.unsqueeze(2).to_broadcast([P, ap.shape[1], E])

                for b, some in enumerate(score_batches(k)):
                    w = some.stop - some.start
                    dve.wait_ge(logits_done, logits_base[k] + some.stop // R)
                    done(nc.vector.tensor_tensor(
                        logits[:, some, :],
                        bank[LOGIT_BANKS[b]][:, 0:w * QUARTER].rearrange("p (t e) -> p t e", e=QUARTER)[:, :, 0:E],
                        per_expert(gate_b_sb[:], w), ALU.add))
                    own()
                    done(nc.vector.tensor_reduce(top[:, some], logits[:, some], AX.X, ALU.max))
                    own()
                    done(nc.vector.tensor_tensor(hit[:, some], logits[:, some], per_token(top[:, some]), ALU.is_ge))
                    own()
                    done(nc.vector.tensor_tensor(hit[:, some], hit[:, some], per_expert(expert_iota, w), ALU.mult))
                    own()
                    done(nc.vector.tensor_reduce(first[:, some], hit[:, some], AX.X, ALU.min))
                    own()
                    nc.vector.tensor_tensor(onehot[:, some], per_expert(expert_iota, w), per_token(first[:, some]),
                                            ALU.is_equal).then_inc(onehot_ready, 1)

            def place_rows(k):
                tg = groups[k][1] * R
                t = slice(0, tg)
                dve.wait_ge(ranks_done, route_phase[k] + 1)
                ranks = bank[RANK_BANK][:, 0:(tg + 1) * E].rearrange("p (t e) -> p t e", e=E)
                done(nc.vector.tensor_scalar(tiles_i[:], ranks[:, tg, :], float(P - 1), None, ALU.add))
                own()
                done(nc.vector.tensor_scalar(tiles_i[:], tiles_i[:], P.bit_length() - 1, None,
                                             ALU.arith_shift_right))
                own()
                done(nc.vector.scalar_tensor_tensor(
                    out=starts_m[:], in0=tiles_i[:].unsqueeze(1).to_broadcast([P, E + 1, E]), scalar=1.0,
                    in1=lower, op0=ALU.max, op1=ALU.mult))
                own()
                done(nc.vector.tensor_reduce(starts_f[:], starts_m[:], AX.X, ALU.add))
                own()
                done(nc.vector.scalar_tensor_tensor(out=place[:, t], in0=per_expert(starts_f[:, 0:E], tg), scalar=float(P),
                                                    in1=ranks[:, 0:tg, :], op0=ALU.mult, op1=ALU.add))
                done(nc.vector.tensor_copy(starts[k][:], starts_f[:]))
                own()
                done(nc.vector.tensor_tensor(place[:, t], place[:, t], onehot[:, t], ALU.mult))
                own()
                done(nc.vector.tensor_reduce(rows_f[:, t], place[:, t], AX.X, ALU.add))
                own()
                nc.vector.tensor_copy(rows[k][:], rows_f[:, t]).then_inc(routed, 1)

            def experts(k, bounds, between=None):
                dve.wait_ge(halved, 2)
                own()
                dve.sem_inc(y_copied[k], 1)
                dve.sem_inc(relu_v[k], HC // 2)

                tiles_b = tiles[groups[k][2]]

                def stage(i):
                    dve.wait_ge(tiles_loaded[k], 16 * (i // QUAD + 1))
                    nc.vector.tensor_copy(x_stage[:].unsqueeze(1), tiles_b[:, bass.ds(i, 1), :]).then_inc(x_staged[k], 1)

                def relu(i, e):
                    for c in range(HC // 2, HC):
                        dve.wait_ge(h_done[k], HC * i + c + 1)
                        nc.vector.tensor_scalar(hT[:, c, :], bank[c][:, 0:P], b1_sb[:, e * HC + c:e * HC + c + 1], 0.0,
                                                ALU.add, ALU.max).then_inc(relu_v[k], 1)
                    dve.wait_ge(xT_done[k], i + 2)
                    stage(i + 2)

                def take_output(following, e):
                    dve.wait_ge(y_done[k], following)
                    nc.vector.tensor_tensor(tiles_b[:, bass.ds(following - 1, 1), :], bank[4][:, 0:D].unsqueeze(1),
                                            b2_sb[:, e:e + 1, :], ALU.add).then_inc(y_copied[k], 1)

                stage(0)
                dve.wait_ge(xT_done[k], 1)
                stage(1)
                relu(0, 0)
                for e in range(E):
                    with dve.Fori(bounds[e] + 1, bounds[e + 1]) as i:
                        take_output(i, e)
                        relu(i, e)
                    take_output(bounds[e + 1], e)
                    if e + 1 < E:
                        relu(bounds[e + 1], e + 1)
                    if between:
                        between(e)
                dve.wait_ge(x_staged[k], bounds[E] + AHEAD)
                dve.sem_inc(v_phases, 1)

            def attn_moments(c):
                dve.wait_ge(ffn_added[c], 1)
                moments("attn", c)

            def first_attn(e):
                lo, hi = [min(max(0, i - FIRST_MOMENTS) * HEAD // (FIRST_NORM + 1 - FIRST_MOMENTS), HEAD)
                          for i in (e, e + 1)]
                for c in range(lo, hi):
                    attn_moments(c)
                if e == FIRST_NORM:
                    variance(("attn", 0))
                if e == FIRST_NORM + 1:
                    invert(("attn", 0))

            def attention(at, chunks, meanwhile=lambda: None):
                def take_qkv(j):
                    n = at + j
                    dve.wait_ge(qkv_done, n + 1)
                    qkv = bank[1][:, 0:R * QKV].rearrange("p (r n) -> p r n", r=R)
                    nc.vector.tensor_tensor(qk[:].rearrange("p s r n -> p r s n"),
                                            qkv[:, :, 0:2 * CLASS_CH].rearrange("p r (s n) -> p r s n", s=2),
                                            bqkv_sb[:, :, 0:2 * CLASS_CH].rearrange("p r (s n) -> p r s n", s=2),
                                            ALU.add).then_inc(qk_ready, 1)
                    for b in range(2):
                        s = slice(b * SEQ, (b + 1) * SEQ)
                        for h in range(2):
                            col = h * (HEAD_DIM + 1)

                            def pair(ap):
                                return ap[s, :, 2 * CLASS_CH:].rearrange("p r (w h d) -> p r w h d", h=2,
                                                                         d=HEAD_DIM)[:, :, :, h, :]

                            last = nc.vector.tensor_tensor(
                                v_pairs[h * SEQ:(h + 1) * SEQ, n % V_SLOTS, :, :, b, col:col + HEAD_DIM],
                                pair(qkv), pair(bqkv_sb), ALU.add)
                    last.then_inc(v_ready, 1)

                def shift(j):
                    n = at + j
                    for s in range(2):
                        dve.wait_ge(scores_done, 2 * n + s + 1)
                        sc = bank[4 + s][:, :].rearrange("p (h q) -> p h q", q=SEQ)
                        m = row_max[:, 8 * s:8 * s + 8]
                        done(nc.vector.tensor_reduce(m, sc, AX.X, ALU.max))
                        own()
                        nc.vector.tensor_tensor(
                            probs[:, n % 2, 2 * s:2 * s + 2, :].rearrange("p r (h q) -> p (r h) q", q=SEQ), sc,
                            m.unsqueeze(2).to_broadcast([P, 8, SEQ]), ALU.subtract).then_inc(shifted, 1)

                def attend(j):
                    n = at + j
                    dve.wait_ge(ctx_done, n + 1)
                    got = bank[1][:, 0:R * ROWS * PAIR].rearrange("p (w d) -> p w d", d=HEAD_DIM + 1)
                    done(nc.vector.reciprocal(inv_sum[:], got[:, :, HEAD_DIM]))
                    own()
                    nc.vector.tensor_tensor(attended[:], got[:, :, 0:HEAD_DIM],
                                            inv_sum[:].unsqueeze(2).to_broadcast([P, R * CLASS_HEADS, HEAD_DIM]),
                                            ALU.mult).then_inc(ctx_used, 1)
                    dve.wait_ge(ctx_used, n + 1)
                    chunk = x_sb[:, n, :]
                    mine = bass.AP(chunk.tensor, chunk.offset, [chunk.ap[0], [D + HEAD_DIM, R], [R * HEAD_DIM, CLASS_HEADS],
                                                                [1, HEAD_DIM]])
                    done(nc.vector.tensor_tensor(mine, mine, attended[:].rearrange("p (r h) d -> p r h d", r=R), ALU.add))
                    own()
                    moments("ffn1", n)

                take_qkv(0)
                meanwhile()
                take_qkv(1)
                shift(0)
                for j in range(chunks):
                    if HEAD <= at + j + 3 < MAIN:
                        scale(dve, "attn", j + 3)
                    if j + 2 < chunks:
                        take_qkv(j + 2)
                    if j + 1 < chunks:
                        shift(j + 1)
                    for step in deviations[at].get(j, ()):
                        invert(step)
                    attend(j)
                    for c in late_moments[at].get(j, ()):
                        attn_moments(c)
                    for step in deviations[at].get(j + 1, ()):
                        variance(step)

            def first_moments(at, chunks):
                for c in range(at, at + chunks):
                    dve.wait_ge(x_loaded[c * XL // CHUNKS], 16)
                    moments("ffn0", c)

            first_moments(0, HEAD)
            normalise(("ffn0", 0))
            first_moments(HEAD, EARLY)
            dve.wait_ge(weights_loaded, 64)
            pick((0, 0))
            place_rows((0, 0))
            first_moments(HEAD + EARLY, CHUNKS - HEAD - EARLY)
            normalise(("ffn0", HEAD))
            bounds = expert_bounds(dve, (0, 0))
            pick((0, 1))
            place_rows((0, 1))
            next_bounds = [0]
            experts((0, 0), bounds, lambda e: next_bounds.append(end_of(dve, (0, 1), e)))
            experts((0, 1), next_bounds, first_attn)
            attention(*attention_runs[0])
            normalise(("ffn1", HEAD))
            for c in range(MAIN, CHUNKS):
                scale(dve, "attn", c)
            pick((1, 0))
            attention(*attention_runs[1], lambda: place_rows((1, 0)))
            normalise(("ffn1", MAIN + TAIL // 2))
            bounds = expert_bounds(dve, (1, 0))
            pick((1, 1))
            place_rows((1, 1))
            next_bounds = [0]
            experts((1, 0), bounds, lambda e: next_bounds.append(end_of(dve, (1, 1), e)))
            experts((1, 1), next_bounds)
            at, chunks, _ = groups[1, 1]
            for c in range(at, at + chunks):
                add_ffn(dve, 1, c)

        @block.tensor
        def _(pe):
            def transpose_xn(use, c, banks=1):
                n = norm_at[use, c]
                pe.wait_ge(xn_ready[c], norm_round[use])
                if n >= banks:
                    pe.wait_ge(xnT_copied, n + 1 - banks)
                for r in range(R):
                    last = nc.tensor.transpose(bank[n % banks][:, r * P:(r + 1) * P], xn_sb[:, c, r, :], ident)
                last.then_inc(xnT_done, 1)

            def gate(k):
                at, chunks, _ = groups[k]
                use = f"ffn{k[0]}"
                base = norm_at[use, at]
                scored = logits_base[k]
                for j in range(chunks + 2):
                    if j < chunks:
                        transpose_xn(use, at + j, GATE_BANKS)
                    if 1 <= j <= chunks:
                        i = j - 1
                        pe.wait_ge(xnT_copied, base + i + 1)
                        for r in range(R):
                            last = nc.tensor.matmul(bank[(2, 5)[i % 2]][r * QUARTER:(r + 1) * QUARTER, 0:P],
                                                    gate_sb[:], xnT[:, (base + i) % 2, r, :], start=True, stop=True)
                        last.then_inc(logitsT_done, 1)
                    if j >= 2:
                        i = j - 2
                        pe.wait_ge(logitsT_copied, scored + i + 1)
                        nc.tensor.transpose(bank[LOGIT_BANKS[i // 4]][:, i % 4 * P:(i % 4 + 1) * P],
                                            logitsT[:, i % 2, :], ident).then_inc(logits_done, 1)

            def rank(k):
                tg = groups[k][1] * R
                for b, some in enumerate(score_batches(k)):
                    pe.wait_ge(onehot_ready, onehot_base[k] + b + 1)
                    for t in range(some.start, some.stop):
                        last = nc.tensor.matmul(bank[RANK_BANK][:, (t + 1) * E:(tg + 1) * E].rearrange("p (t e) -> p t e", e=E),
                                                ones[:], onehot[:, t:t + 1, :].to_broadcast([P, tg - t, E]),
                                                start=(t == 0), stop=(t == tg - 1), skip_group_check=True)
                        if t == some.start:
                            nc.tensor.matmul(bank[RANK_BANK][:, some.start * E:some.stop * E], tri[:],
                                             onehot[:, some].rearrange("p t e -> p (t e)"),
                                             start=False, stop=False, skip_group_check=True)
                last.then_inc(ranks_done, 1)

            def experts(k, bounds, between=None):
                pe.wait_ge(halved, 2)
                pe.wait_ge(routed, 2 * k[0] + 2)

                def transpose_x(i):
                    pe.wait_ge(x_staged[k], i + 1)
                    nc.tensor.transpose(bank[6][:, 0:P], x_stage[:], ident).then_inc(xT_done[k], 1)

                def hidden(i, e):
                    pe.wait_ge(xT_copied[k], i + 1)
                    for c in range(HC):
                        nc.tensor.matmul(bank[c][:, 0:P], w1_sb[:, e, c * P:(c + 1) * P], xT[:],
                                         start=True, stop=True).then_inc(h_done[k], 1)
                    transpose_x(i + 1)

                def output(following, e):
                    pe.wait_ge(y_copied[k], following)
                    for c in range(HC):
                        pe.wait_ge(relu_a[k] if c < HC // 2 else relu_v[k], HC // 2 * following + c % (HC // 2) + 1)
                        last = nc.tensor.matmul(bank[4][:, 0:D], hT[:, c, :], w2_sb[:, e, c, :],
                                                start=(c == 0), stop=(c == HC - 1))
                    last.then_inc(y_done[k], 1)

                transpose_x(0)
                hidden(0, 0)
                for e in range(E):
                    with pe.Fori(bounds[e] + 1, bounds[e + 1]) as i:
                        output(i, e)
                        hidden(i, e)
                    output(bounds[e + 1], e)
                    if e + 1 < E:
                        hidden(bounds[e + 1], e + 1)
                    if between:
                        between(e)
                pe.wait_ge(xT_copied[k], bounds[E] + 1)
                pe.sem_inc(pe_phases, 1)

            def attention(at, chunks, meanwhile=lambda: None, after=lambda j: None):
                base = norm_at["attn", at]

                def project(j):
                    n = base + j
                    m = at + j
                    pe.wait_ge(xnT_copied, n + 1)
                    if m >= 1:
                        pe.wait_ge(v_ready, m)
                    if j >= 3:
                        pe.wait_ge(ctx_used, m - 2)
                    for r in range(R):
                        last = nc.tensor.matmul(bank[1][:, r * QKV:(r + 1) * QKV], xnT[:, n % 2, r, :],
                                                wqkv_sb[:, r, :], start=True, stop=True)
                    last.then_inc(qkv_done, 1)

                def transpose_qk(j):
                    pe.wait_ge(qk_ready, at + j + 1)
                    for s, done in ((0, qT_done), (1, kT_done)):
                        nc.tensor.transpose(bank[2 + s][:, 0:P], qk[:, s, :, :].rearrange("p r n -> p (r n)"),
                                            ident).then_inc(done, 1)

                def scores(j):
                    n = at + j
                    pe.wait_ge(q_ready, n + 1)
                    pe.wait_ge(k_ready, n + 1)
                    for r in range(R):
                        if n >= 1 and r % 2 == 0:
                            pe.wait_ge(shifted, 2 * n - 1 + r // 2)
                        for b in range(2):
                            s = slice(b * SEQ, (b + 1) * SEQ)
                            last = nc.tensor.matmul(bank[4 + r // 2][s, (r % 2) * 256:(r % 2) * 256 + 256],
                                                    q_by_class[:, r, s], k_by_head[:, :, s], start=True, stop=True)
                        if r % 2:
                            last.then_inc(scores_done, 1)

                def transpose_probs(j):
                    n = at + j
                    for s in range(2):
                        pe.wait_ge(exp_done, 2 * n + s + 1)
                        for u in range(4):
                            r, w = 2 * s + u // 2, u % 2
                            last = nc.tensor.transpose(bank[6 + s][:, u * P:(u + 1) * P],
                                                       probs[:, n % 2, r, w * P:(w + 1) * P], ident)
                        last.then_inc(probsT_done, 1)

                def weigh_values(j):
                    n = at + j
                    pe.wait_ge(v_ready, min(n + 3, at + chunks))
                    if j >= chunks - 2:
                        pe.wait_ge(ctx_used, n)
                    for s in range(2):
                        pe.wait_ge(probsT_copied, 2 * n + s + 1)
                        for u in range(4 * s, 4 * s + 4):
                            for b in range(2):
                                q = slice(b * SEQ, (b + 1) * SEQ)
                                last = nc.tensor.matmul(bank[1][q, u * PAIR:(u + 1) * PAIR], probsT[:, u, q],
                                                        v_pairs[:, n % V_SLOTS, u // ROWS, u % ROWS, b, :],
                                                        start=True, stop=True)
                    last.then_inc(ctx_done, 1)

                transpose_xn("attn", at)
                transpose_xn("attn", at + 1)
                project(0)
                meanwhile()
                transpose_qk(0)
                project(1)
                scores(0)
                transpose_qk(1)
                for j in range(chunks):
                    if j + 2 < chunks:
                        transpose_xn("attn", at + j + 2)
                    if j + 1 < chunks:
                        scores(j + 1)
                    if j + 2 < chunks:
                        project(j + 2)
                    transpose_probs(j)
                    if j + 2 < chunks:
                        transpose_qk(j + 2)
                    weigh_values(j)
                    after(j)
                pe.wait_ge(ctx_used, at + chunks)

            def load_bounds(j):
                for e in range(j * E // TAIL, (j + 1) * E // TAIL):
                    bounds.append(end_of(pe, (1, 0), e))

            pe.wait_ge(consts_loaded, 16)
            pe.wait_ge(weights_loaded, 64)
            gate((0, 0))
            rank((0, 0))
            gate((0, 1))
            rank((0, 1))
            next_bounds = [0]
            experts((0, 0), expert_bounds(pe, (0, 0)), lambda e: next_bounds.append(end_of(pe, (0, 1), e)))
            experts((0, 1), next_bounds)
            pe.wait_ge(consts_ready, 1)
            attention(*attention_runs[0])
            gate((1, 0))
            bounds = [0]
            attention(*attention_runs[1], lambda: rank((1, 0)), load_bounds)
            gate((1, 1))
            rank((1, 1))
            next_bounds = [0]
            experts((1, 0), bounds, lambda e: next_bounds.append(end_of(pe, (1, 1), e)))
            experts((1, 1), next_bounds)


def kernel(L0_attn_X, L0_attn_Wq, L0_attn_bq, L0_attn_Wkv, L0_attn_bkv, L0_ffn_gate_w, L0_ffn_gate_b,
           L0_ffn_w1, L0_ffn_b1, L0_ffn_w2, L0_ffn_b2):
    import concourse.bacc as bacc
    from concourse.bass_utils import run_bass_kernel_spmd

    shape = np.shape(L0_attn_X)
    d = shape[-1]
    e, hid, _ = np.shape(L0_ffn_w1)

    def by_class(w, parts):
        w = np.asarray(w).reshape(-1, parts, CLASS_HEADS, R, HEAD_DIM)
        return w.transpose(0, 3, 1, 2, 4).reshape(-1, R, parts * CLASS_CH)

    arrays = {
        "x": np.asarray(L0_attn_X).reshape(-1, d),
        "w_qkv": np.concatenate([by_class(L0_attn_Wq, 1), by_class(L0_attn_Wkv, 2)], axis=2),
        "b_qkv": np.concatenate([by_class(L0_attn_bq, 1), by_class(L0_attn_bkv, 2)], axis=2)[0],
        "gate_w": np.asarray(L0_ffn_gate_w).T,
        "gate_b": np.asarray(L0_ffn_gate_b),
        "w1": np.asarray(L0_ffn_w1).transpose(2, 0, 1),
        "b1": np.asarray(L0_ffn_b1).reshape(e * hid // P, P).T,
        "w2": np.asarray(L0_ffn_w2).reshape(e, d, hid // P, P).transpose(3, 0, 2, 1),
        "b2": np.asarray(L0_ffn_b2),
        "consts": shape_constants(e),
    }
    nc = bacc.Bacc("TRN2", target_bir_lowering=False, num_devices=1)
    maps, args = {}, []
    for name, a in arrays.items():
        a = np.ascontiguousarray(a)
        maps[f"in_{name}"] = a
        args.append(nc.dram_tensor(f"in_{name}", a.shape, mybir.dt.from_np(a.dtype), kind="ExternalInput").ap())
    args.append(nc.dram_tensor("out_x", arrays["x"].shape, F32, kind="ExternalOutput").ap())
    macaron_kernel(nc, *args)
    got = run_bass_kernel_spmd(nc, [maps], core_ids=[0])
    return got.results[0]["out_x"].reshape(shape)
```

```python
from contextlib import ExitStack

import numpy as np

import concourse.bass as bass
from concourse import mybir

ALU = mybir.AluOpType
ACT = mybir.ActivationFunctionType
AX = mybir.AxisListType
F32 = mybir.dt.float32
BF16 = mybir.dt.bfloat16
I32 = mybir.dt.int32
U32 = mybir.dt.uint32

P = 128
HEADS, HEAD_DIM, R = 16, 8, 4
CLASS_HEADS = HEADS // R
CLASS_CH = CLASS_HEADS * HEAD_DIM
ROWS = CLASS_HEADS // 2
PAIR = 2 * (HEAD_DIM + 1)

C_IDENT, C_TRI, C_IOTA, C_LOWER, C_HEAD, C_END = 0, 128, 256, 264, 336, 340


def shape_constants(experts):
    c = np.zeros((P, C_END), np.float32)
    k = np.arange(P)
    c[:, C_IDENT:C_IDENT + P] = k[:, None] == k[None, :]
    c[:, C_TRI:C_TRI + P] = k[:, None] < k[None, :]
    e = np.arange(experts)
    c[:, C_IOTA:C_IOTA + experts] = e - experts
    c[:, C_LOWER:C_LOWER + (experts + 1) * experts] = (e[None, :] < np.arange(experts + 1)[:, None]).reshape(1, -1)
    c[:, C_HEAD:C_HEAD + CLASS_HEADS] = (k[:, None] % CLASS_CH) // HEAD_DIM == np.arange(CLASS_HEADS)[None, :]
    return c


def macaron_kernel(nc, x, w_qkv, b_qkv, gate_w, gate_b, w1, b1, w2, b2, consts, out):
    TOKENS, D = x.shape
    E = gate_w.shape[1]
    HID = w1.shape[2]
    HC = HID // P
    CHUNKS = TOKENS // (P * R)
    HEAD = CHUNKS * 3 // 8
    TAIL = CHUNKS * 3 // 8
    MAIN = CHUNKS - TAIL
    groups = {(0, 0): (0, HEAD, 0), (0, 1): (HEAD, CHUNKS - HEAD, 1), (1, 0): (0, MAIN, 1), (1, 1): (MAIN, TAIL, 0)}
    phases = list(groups)
    norms = {("ffn0", 0): HEAD, ("ffn0", HEAD): CHUNKS - HEAD, ("attn", 0): HEAD, ("attn", HEAD): 2,
             ("attn", HEAD + 2): MAIN - HEAD - 2, ("ffn1", 0): HEAD, ("attn", MAIN): TAIL,
             ("ffn1", HEAD): MAIN - HEAD, ("ffn1", MAIN): TAIL}
    TG_MAX = max(chunks for _, chunks, _ in groups.values()) * R
    SEQ = P // 2
    QUARTER = P // R
    LOGIT_BANKS, RANK_BANK = (4, 6, 3), 7
    LOGIT_T_BANKS = (2, 5)
    GATE_BANKS = 2
    AHEAD = 2
    QUAD, EARLY_QUADS = 4, 2
    LEAST = 2
    sizes = [[chunks * R for _, chunks, buffer in groups.values() if buffer == b] for b in range(2)]
    MIN_TILES = [min(n) for n in sizes]
    MAX_TILES = [max(n) + LEAST * E for n in sizes]
    LOADED_TILES = [-(-(n + AHEAD) // QUAD) * QUAD for n in MAX_TILES]
    ROWS_CAP = [n * P for n in LOADED_TILES]
    EPS = 1e-5
    FILLS, SPARES = 4, 2
    FILL = [n * D // P // FILLS for n in ROWS_CAP]
    SCALE = float(1.0 / np.sqrt(HEAD_DIM))
    QKV = 3 * CLASS_CH

    sorted_in = [nc.dram_tensor(f"sorted_in{b}", (ROWS_CAP[b], D), F32, kind="Internal").ap() for b in range(2)]
    sorted_out = [nc.dram_tensor(f"sorted_out{b}", (MAX_TILES[b] * P, D), F32, kind="Internal").ap()
                  for b in range(2)]
    x_chunks = x.rearrange("(c p r) d -> p c (r d)", p=P, r=R)
    out_chunks = out.rearrange("(c p r) d -> p c (r d)", p=P, r=R)

    with ExitStack() as ctx:
        def sb(name, shape, dt=F32):
            return ctx.enter_context(nc.sbuf_tensor(name, shape, dt))

        def sem(name):
            return ctx.enter_context(nc.semaphore(name))

        bank = [ctx.enter_context(nc.psum_tensor(f"bank{i}", [P, 512], F32)) for i in range(8)]

        cst = sb("cst", [P, C_END])
        ident = cst[:, C_IDENT:C_IDENT + P]
        expert_iota = cst[:, C_IOTA:C_IOTA + E]
        lower = cst[:, C_LOWER:C_LOWER + (E + 1) * E].rearrange("p (i e) -> p i e", e=E)
        head_mask = cst[:, C_HEAD:C_HEAD + CLASS_HEADS]
        tri = sb("tri", [P, P], BF16)
        ones = sb("ones", [P, P], BF16)
        w1_sb = sb("w1_sb", [P, E, HID])
        w2_sb = sb("w2_sb", [P, E, HC, D])
        b1_sb = sb("b1_sb", [P, E * HC])
        b2_sb = sb("b2_sb", [P, E, D])
        gate_sb = sb("gate_sb", [P, QUARTER])
        gate_b_sb = sb("gate_b_sb", [P, E])
        wqkv_sb = sb("wqkv_sb", [P, R, QKV])
        bqkv_sb = sb("bqkv_sb", [P, R, QKV])
        x_sb = sb("x_sb", [P, CHUNKS, R * D])
        xn_sb = sb("xn_sb", [P, CHUNKS, R, D])
        kinds = {"attn": "attn", "ffn0": "ffn", "ffn1": "ffn"}
        by_use = {name: {kind: sb(f"{name}_{kind}", shape) for kind in ("attn", "ffn")} for name, shape in
                  (("stats", [P, CHUNKS * R, 6]), ("mean", [P, CHUNKS * R]), ("rstd", [P, CHUNKS * R]),
                   ("offset", [P, CHUNKS * R]))}
        stats, mean, rstd, offset = ({use: by_use[name][kind] for use, kind in kinds.items()}
                                     for name in ("stats", "mean", "rstd", "offset"))
        var = sb("var", [P, TG_MAX])
        diff = sb("diff", [P, TG_MAX])
        m2 = sb("m2", [P, TG_MAX])
        std = sb("std", [P, TG_MAX])
        xnT = sb("xnT", [P, 2, R, P])
        logitsT = sb("logitsT", [P, 2, P])
        logits = sb("logits", [P, TG_MAX, E])
        top = sb("top", [P, TG_MAX])
        hit = sb("hit", [P, TG_MAX, E])
        first = sb("first", [P, TG_MAX])
        onehot = sb("onehot", [P, TG_MAX, E], BF16)
        place = sb("place", [P, TG_MAX, E])
        tiles_i = sb("tiles_i", [P, E], I32)
        starts_m = sb("starts_m", [P, E + 1, E])
        starts_f = sb("starts_f", [P, E + 1])
        starts = {k: sb(f"starts_{k[0]}{k[1]}", [P, E + 1], I32) for k in phases}
        rows_f = sb("rows_f", [P, TG_MAX])
        rows = {k: sb(f"rows_{k[0]}{k[1]}", [P, groups[k][1] * R], U32) for k in phases}
        zeros = sb("zeros", [P, max(FILL)])
        tiles = [sb(f"tiles{b}", [P, LOADED_TILES[b], D]) for b in range(2)]
        x_stage = sb("x_stage", [P, D])
        xT = sb("xT", [P, P])
        hT = sb("hT", [P, HC, P])
        V_SLOTS = 3
        qk = sb("qk", [P, 2, R, CLASS_CH])
        q_by_class = sb("q_by_class", [P, R, P])
        k_by_head = sb("k_by_head", [P, CLASS_HEADS, P])
        v_pairs = sb("v_pairs", [P, V_SLOTS, R, ROWS, 2, PAIR])
        row_max = sb("row_max", [P, R * CLASS_HEADS])
        probs = sb("probs", [P, 2, R, CLASS_HEADS * SEQ])
        probsT = sb("probsT", [P, R * ROWS, P])
        inv_sum = sb("inv_sum", [P, R * CLASS_HEADS])
        attended = sb("attended", [P, R * CLASS_HEADS, HEAD_DIM])

        consts_loaded, weights_loaded = sem("consts_loaded"), sem("weights_loaded")
        XL = 8
        x_loaded = [sem(f"x_loaded{i}") for i in range(XL)]
        experts_loaded, halved = sem("experts_loaded"), sem("halved")
        gate_cleared = sem("gate_cleared")
        zeros_ready = sem("zeros_ready")
        padded = [sem(f"padded{b}") for b in range(2)]
        spares_filled = sem("spares_filled")
        blocks_cleared = sem("blocks_cleared")
        v_done = sem("v_done")
        var_ready, std_ready = sem("var_ready"), sem("std_ready")
        rstd_ready = sem("rstd_ready")
        xn_ready = [sem(f"xn_ready{c}") for c in range(CHUNKS)]
        xnT_done, xnT_copied = sem("xnT_done"), sem("xnT_copied")
        logitsT_done, logitsT_copied = sem("logitsT_done"), sem("logitsT_copied")
        logits_done, onehot_ready, ranks_done = sem("logits_done"), sem("onehot_ready"), sem("ranks_done")
        routed = sem("routed")
        scattered = {k: sem(f"scattered_{k[0]}{k[1]}") for k in phases}
        tiles_loaded = {k: sem(f"tiles_loaded_{k[0]}{k[1]}") for k in phases}
        early_loaded = {k: sem(f"early_loaded_{k[0]}{k[1]}") for k in phases if k[1] == 1}
        x_staged = {k: sem(f"x_staged_{k[0]}{k[1]}") for k in phases}
        xT_done = {k: sem(f"xT_done_{k[0]}{k[1]}") for k in phases}
        xT_copied = {k: sem(f"xT_copied_{k[0]}{k[1]}") for k in phases}
        h_done = {k: sem(f"h_done_{k[0]}{k[1]}") for k in phases}
        relu_v = {k: sem(f"relu_v_{k[0]}{k[1]}") for k in phases}
        relu_a = {k: sem(f"relu_a_{k[0]}{k[1]}") for k in phases}
        y_done = {k: sem(f"y_done_{k[0]}{k[1]}") for k in phases}
        y_copied = {k: sem(f"y_copied_{k[0]}{k[1]}") for k in phases}
        y_stored = {k: sem(f"y_stored_{k[0]}{k[1]}") for k in phases}
        gather_begun, pe_finished, v_finished = sem("gather_begun"), sem("pe_finished"), sem("v_finished")
        gathered = [sem(f"gathered{c}") for c in range(CHUNKS)]
        ffn_added = [sem(f"ffn_added{c}") for c in range(CHUNKS)]
        qkv_done, qk_ready, v_ready = sem("qkv_done"), sem("qk_ready"), sem("v_ready")
        qT_done, q_ready, kT_done, k_ready = sem("qT_done"), sem("q_ready"), sem("kT_done"), sem("k_ready")
        scores_done, shifted, exp_done = sem("scores_done"), sem("shifted"), sem("exp_done")
        probsT_done, probsT_copied = sem("probsT_done"), sem("probsT_copied")
        ctx_done, ctx_used = sem("ctx_done"), sem("ctx_used")
        out_stored = sem("out_stored")

        block = ctx.enter_context(nc.Block())

        norm_phase = {step: i for i, step in enumerate(norms)}
        transposed = [("ffn0", 0, CHUNKS), ("attn", 0, MAIN), ("ffn1", 0, MAIN), ("attn", MAIN, TAIL),
                      ("ffn1", MAIN, TAIL)]
        norm_at = {step: i for i, step in enumerate(
            (use, at + j) for use, at, chunks in transposed for j in range(chunks))}
        batch_of = {(use, at + j): (use, at) for (use, at), chunks in norms.items() for j in range(chunks)}
        norm_round = {"ffn0": 1, "attn": 2, "ffn1": 3}
        deviations = {0: {HEAD - 4: [("attn", HEAD)], HEAD - 2: [("attn", HEAD + 2)], HEAD: [("ffn1", 0)],
                          MAIN - 1: [("attn", MAIN)]},
                      MAIN: {}}
        late_moments = {0: {}, MAIN: {}}
        for c in range(HEAD, MAIN):
            late_moments[0].setdefault(c - HEAD, []).append(c)
        for c in range(MAIN, CHUNKS):
            late_moments[0].setdefault(min(MAIN - HEAD + c - MAIN, MAIN - 2), []).append(c)
        FIRST_NORM = E // 2
        ACT_SCALED = {0: HEAD - 2, 2: HEAD - 1}
        ACT_SCALED_LAST = {0: CHUNKS - 2, 2: CHUNKS - 1}
        POOL_SCALED = 5
        EARLY = (CHUNKS - HEAD) // 2

        def score_batches(k):
            tg = groups[k][1] * R
            return [slice(i, min(tg, i + 4 * R)) for i in range(0, tg, 4 * R)]

        onehot_base = {k: sum(len(score_batches(p)) for p in phases[:i]) for i, k in enumerate(phases)}
        logits_base = {k: sum(groups[p][1] for p in phases[:i]) for i, k in enumerate(phases)}
        route_phase = {k: i for i, k in enumerate(phases)}
        attention_runs = [(0, MAIN), (MAIN, TAIL)]

        def end_of(eng, k, e):
            eng.wait_ge(routed, route_phase[k] + 1)
            return eng.value_load(starts[k][0:1, e + 1:e + 2], min_val=LEAST * (e + 1),
                                  max_val=MAX_TILES[groups[k][2]])

        def expert_bounds(eng, k):
            return [0] + [end_of(eng, k, e) for e in range(E)]

        def expert_total(eng, k):
            return eng.value_load(starts[k][0:1, E:E + 1], min_val=LEAST * E, max_val=MAX_TILES[groups[k][2]])

        def add_ffn(eng, f, c):
            eng.wait_ge(gathered[c], 16 * R * (f + 1))
            eng.tensor_tensor(x_sb[:, c, :], x_sb[:, c, :], xn_sb[:, c, :, :].rearrange("p r d -> p (r d)"),
                              ALU.add).then_inc(ffn_added[c], 1)

        def scale(eng, use, c):
            for r in range(R):
                i = c * R + r
                last = eng.tensor_scalar(xn_sb[:, c, r, :], x_sb[:, c, r * D:(r + 1) * D], mean[use][:, i:i + 1],
                                         rstd[use][:, i:i + 1], ALU.subtract, ALU.mult)
            last.then_inc(xn_ready[c], 1)

        @block.sync
        def _(sp):
            per = CHUNKS // XL
            for i in range(XL):
                sp.dma_start(x_sb[:, i * per:(i + 1) * per, :],
                             x_chunks[:, i * per:(i + 1) * per, :]).then_inc(x_loaded[i], 16)

            def pad(b):
                fill = sorted_in[b].rearrange("(n p k) d -> n p (k d)", p=P, n=FILLS)
                for n in range(FILLS):
                    sp.dma_start(fill[n], zeros[:, 0:FILL[b]]).then_inc(padded[b], 16)

            sp.wait_ge(zeros_ready, 1)
            pad(0)
            sp.dma_start(w1_sb[:], w1).then_inc(experts_loaded, 16)
            sp.dma_start(b1_sb[:], b1).then_inc(experts_loaded, 16)
            sp.dma_start(w2_sb[:], w2).then_inc(experts_loaded, 16)
            sp.dma_start(b2_sb[:], b2.partition_broadcast(P)).then_inc(experts_loaded, 16)
            pad(1)
            def fill_spares():
                for b in range(2):
                    spare = sorted_out[b][MIN_TILES[b] * P:MAX_TILES[b] * P, :].rearrange("(p k) d -> p (k d)", p=P)
                    for n in range(SPARES):
                        w = spare.shape[1] // SPARES
                        sp.dma_start(spare[:, n * w:(n + 1) * w], zeros[:, 0:w]).then_inc(spares_filled, 16)

            def load_tiles(k, behind):
                _, chunks, b = groups[k]
                quads_in = sorted_in[b].rearrange("(m q p) d -> m p q d", p=P, q=QUAD)
                sp.wait_ge(scattered[k], 16 * chunks * R)
                total = expert_total(sp, k)
                if not behind:
                    sp.dma_start(tiles[b][:, 0:QUAD, :], quads_in[0]).then_inc(tiles_loaded[k], 16)
                with sp.Fori(behind or 1, (total + (AHEAD + QUAD - 1)) // QUAD) as m:
                    sp.wait_ge(tiles_loaded[k], 16 * m)
                    sp.dma_start(tiles[b][:, bass.ds(QUAD * m, QUAD), :],
                                 quads_in[bass.ds(m, 1)]).then_inc(tiles_loaded[k], 16)

            def store_tiles(k):
                b = groups[k][2]
                tiles_out = sorted_out[b].rearrange("(n p) d -> n p d", p=P)
                with sp.Fori(0, expert_total(sp, k)) as i:
                    sp.wait_ge(y_copied[k], i + 2)
                    sp.dma_start(tiles_out[bass.ds(i, 1)], tiles[b][:, bass.ds(i, 1), :]).then_inc(y_stored[k], 16)

            for f in range(2):
                load_tiles((f, 0), 0)
                if f == 0:
                    fill_spares()
                    sp.wait_ge(spares_filled, 16 * 2 * SPARES)
                store_tiles((f, 0))
                load_tiles((f, 1), EARLY_QUADS)
                store_tiles((f, 1))
            for c in range(CHUNKS):
                sp.wait_ge(ffn_added[c], 2)
                sp.dma_start(out_chunks[:, c, :], x_sb[:, c, :]).then_inc(out_stored, 16)
            sp.wait_ge(out_stored, 16 * CHUNKS)

        @block.gpsimd
        def _(pool):
            nc.gpsimd.memset(gate_sb[:], 0.0).then_inc(gate_cleared, 1)
            nc.gpsimd.memset(zeros[:], 0.0).then_inc(zeros_ready, 1)
            nc.gpsimd.memset(q_by_class[:], 0.0).then_inc(blocks_cleared, 1)
            nc.gpsimd.memset(v_pairs[:], 0.0).then_inc(blocks_cleared, 1)
            pool.wait_ge(blocks_cleared, 2)
            for h in range(2):
                s = slice(h * SEQ, (h + 1) * SEQ)
                at = h * (HEAD_DIM + 1) + HEAD_DIM
                for slot in range(V_SLOTS):
                    columns = v_pairs[s, slot, :, :, :, at:at + 1].rearrange("p r w b o -> p r (w b o)")
                    nc.gpsimd.memset(columns, 1.0).then_inc(blocks_cleared, 1)
            pool.wait_ge(blocks_cleared, 2 + 2 * V_SLOTS)

            def scatter(k):
                at, chunks, b = groups[k]
                pool.wait_ge(routed, route_phase[k] + 1)
                pool.wait_ge(padded[b], 16 * FILLS)
                for t in range(chunks * R):
                    pool.indirect_dma_start(
                        out=sorted_in[b], out_offset=bass.IndirectOffsetOnAxis(ap=rows[k][:, t:t + 1], axis=0),
                        in_=xn_sb[:, at + t // R, t % R, :], in_offset=None).then_inc(scattered[k], 16)

            def gather(k):
                at, chunks, b = groups[k]
                pool.wait_ge(spares_filled, 16 * 2 * SPARES)
                pool.wait_ge(y_stored[k], 16 * expert_total(pool, k))
                pool.sem_inc(gather_begun, 1)
                for j in range(chunks + 1):
                    if j < chunks:
                        for r in range(R):
                            t = j * R + r
                            pool.indirect_dma_start(
                                out=xn_sb[:, at + j, r, :], out_offset=None, in_=sorted_out[b],
                                in_offset=bass.IndirectOffsetOnAxis(ap=rows[k][:, t:t + 1], axis=0),
                            ).then_inc(gathered[at + j], 16)
                    if j >= 1 and k != phases[-1]:
                        add_ffn(pool, k[0], at + j - 1)

            def scale_some(step, chunks):
                pool.wait_ge(rstd_ready, norm_phase[step] + 1)
                for c in range(step[1], step[1] + chunks):
                    scale(pool, step[0], c)

            def load_early(k):
                _, chunks, b = groups[k]
                pool.wait_ge(scattered[k], 16 * chunks * R)
                quads_in = sorted_in[b].rearrange("(m q p) d -> m p q d", p=P, q=QUAD)
                for m in range(EARLY_QUADS):
                    pool.dma_start(tiles[b][:, QUAD * m:QUAD * (m + 1), :],
                                   quads_in[m]).then_inc(early_loaded[k], 16)

            scatter((0, 0))
            scatter((0, 1))
            load_early((0, 1))
            gather((0, 0))
            scale_some(("attn", 0), POOL_SCALED)
            gather((0, 1))
            scale_some(("ffn1", 0), HEAD)
            scale_some(("attn", MAIN), TAIL // 2)
            scatter((1, 0))
            scatter((1, 1))
            load_early((1, 1))
            gather((1, 0))
            gather((1, 1))

        @block.scalar
        def _(act):
            act.dma_start(cst[:], consts).then_inc(consts_loaded, 16)
            act.dma_start(gate_b_sb[:], gate_b.partition_broadcast(P)).then_inc(weights_loaded, 16)
            act.dma_start(wqkv_sb[:], w_qkv).then_inc(weights_loaded, 16)
            act.dma_start(bqkv_sb[:], b_qkv.partition_broadcast(P)).then_inc(weights_loaded, 16)
            act.wait_ge(gate_cleared, 1)
            act.dma_start(gate_sb[:, 0:E], gate_w).then_inc(weights_loaded, 16)

            def deviation(step):
                act.wait_ge(var_ready, norm_phase[step] + 1)
                n = norms[step] * R
                nc.scalar.activation(std[:, 0:n], var[:, 0:n], ACT.Sqrt).then_inc(std_ready, 1)

            def scale_a(use, c):
                act.wait_ge(rstd_ready, norm_phase[batch_of[use, c]] + 1)
                for r in range(R):
                    i = c * R + r
                    last = nc.scalar.activation(xn_sb[:, c, r, :], x_sb[:, c, r * D:(r + 1) * D], ACT.Identity,
                                                bias=offset[use][:, i:i + 1], scale=rstd[use][:, i:i + 1])
                last.then_inc(xn_ready[c], 1)

            def copy_xnT(n, banks=1):
                act.wait_ge(xnT_done, n + 1)
                nc.scalar.activation(xnT[:, n % 2, :, :], bank[n % banks][:, :], ACT.Copy).then_inc(xnT_copied, 1)

            def experts(k, bounds, between=None):
                act.wait_ge(experts_loaded, 64)
                act.sem_inc(relu_a[k], HC // 2)

                def copy_xT(i):
                    act.wait_ge(xT_done[k], i + 1)
                    nc.scalar.activation(xT[:], bank[6][:, 0:P], ACT.Copy).then_inc(xT_copied[k], 1)

                copy_xT(0)
                for e in range(E):
                    with act.Fori(bounds[e], bounds[e + 1]) as i:
                        for c in range(0, HC // 2):
                            act.wait_ge(h_done[k], HC * i + c + 1)
                            nc.scalar.activation(hT[:, c, :], bank[c][:, 0:P], ACT.Relu,
                                                 bias=b1_sb[:, e * HC + c:e * HC + c + 1]).then_inc(relu_a[k], 1)
                        copy_xT(i + 1)
                    if between:
                        between(e)

            def attention(at, chunks):
                base = norm_at["attn", at]

                def split_q(j):
                    act.wait_ge(qT_done, at + j + 1)
                    for r in range(R):
                        s = slice(r * CLASS_CH, (r + 1) * CLASS_CH)
                        last = nc.scalar.activation(q_by_class[s, r, :], bank[2][s, 0:P], ACT.Copy)
                    last.then_inc(q_ready, 1)

                def split_k(j):
                    act.wait_ge(kT_done, at + j + 1)
                    for h in range(CLASS_HEADS):
                        last = nc.scalar.activation(k_by_head[:, h, :], bank[3][:, 0:P], ACT.Copy,
                                                    scale=head_mask[:, h:h + 1])
                    last.then_inc(k_ready, 1)

                def softmax_exp(j):
                    n = at + j
                    for s in range(2):
                        act.wait_ge(shifted, 2 * n + s + 1)
                        part = probs[:, n % 2, 2 * s:2 * s + 2, :]
                        nc.scalar.activation(part, part, ACT.Exp, scale=SCALE).then_inc(exp_done, 1)

                def copy_probsT(j):
                    n = at + j
                    for s in range(2):
                        act.wait_ge(probsT_done, 2 * n + s + 1)
                        nc.scalar.activation(probsT[:, 4 * s:4 * s + 4, :], bank[6 + s][:, :],
                                             ACT.Copy).then_inc(probsT_copied, 1)

                copy_xnT(base)
                copy_xnT(base + 1)
                for j in range(2):
                    split_q(j)
                    split_k(j)
                softmax_exp(0)
                for j in range(chunks):
                    if j + 2 < chunks:
                        copy_xnT(base + j + 2)
                    if POOL_SCALED <= at + j + 3 < MAIN:
                        scale_a("attn", at + j + 3)
                    copy_probsT(j)
                    for step in deviations[at].get(j, ()):
                        deviation(step)
                    if j + 2 < chunks:
                        split_q(j + 2)
                        split_k(j + 2)
                    if j + 1 < chunks:
                        softmax_exp(j + 1)

            def gate(k, inside=(), scaled=None):
                at, chunks, _ = groups[k]
                for j in range(chunks + 1):
                    if j == 1:
                        for step in inside:
                            deviation(step)
                    if j < chunks:
                        copy_xnT(norm_at[f"ffn{k[0]}", at + j], GATE_BANKS)
                    if j >= 1:
                        i = j - 1
                        act.wait_ge(logitsT_done, logits_base[k] + i + 1)
                        nc.scalar.activation(logitsT[:, i % 2, :], bank[LOGIT_T_BANKS[i % 2]][:, 0:P],
                                             ACT.Copy).then_inc(logitsT_copied, 1)
                    for use, c in (scaled or {}).get(j, ()):
                        scale_a(use, c)

            def first_attn(e):
                if e == FIRST_NORM:
                    deviation(("attn", 0))

            deviation(("ffn0", 0))
            gate((0, 0), scaled={j: [("ffn0", c)] for j, c in ACT_SCALED.items()})
            deviation(("ffn0", HEAD))
            gate((0, 1))
            act.wait_ge(experts_loaded, 64)
            nc.scalar.activation(w2_sb[:], w2_sb[:], ACT.Copy, scale=0.5).then_inc(halved, 1)
            nc.scalar.activation(b2_sb[:], b2_sb[:], ACT.Copy, scale=0.5).then_inc(halved, 1)
            next_bounds = [0]
            experts((0, 0), expert_bounds(act, (0, 0)), lambda e: next_bounds.append(end_of(act, (0, 1), e)))
            experts((0, 1), next_bounds, first_attn)
            act.wait_ge(blocks_cleared, 2 + 2 * V_SLOTS)
            attention(*attention_runs[0])
            gate((1, 0), [("ffn1", HEAD)])
            attention(*attention_runs[1])
            deviation(("ffn1", MAIN))
            gate((1, 1), scaled={j: [("ffn1", c)] for j, c in ACT_SCALED_LAST.items()})
            next_bounds = [0]
            experts((1, 0), expert_bounds(act, (1, 0)), lambda e: next_bounds.append(end_of(act, (1, 1), e)))
            experts((1, 1), next_bounds)

        @block.vector
        def _(dve):
            count = [0]

            def done(ins):
                count[0] += 1
                return ins.then_inc(v_done, 1)

            def own():
                dve.wait_ge(v_done, count[0])

            dve.wait_ge(consts_loaded, 16)
            done(nc.vector.tensor_copy(tri[:], cst[:, C_TRI:C_TRI + P]))
            done(nc.vector.memset(ones[:], 1.0))

            def moments(use, c):
                for r in range(R):
                    done(nc.vector.bn_stats(stats[use][:, c * R + r, :], x_sb[:, c, r * D:(r + 1) * D]))

            def variance(step):
                use, at = step
                n = norms[step] * R
                t = slice(at * R, at * R + n)
                own()
                mu = mean[use][:, t]
                me, mo = stats[use][:, t, 1], stats[use][:, t, 4]
                done(nc.vector.tensor_tensor(mu, me, mo, ALU.add))
                done(nc.vector.tensor_tensor(diff[:, 0:n], me, mo, ALU.subtract))
                done(nc.vector.tensor_tensor(m2[:, 0:n], stats[use][:, t, 2], stats[use][:, t, 5], ALU.add))
                own()
                done(nc.vector.tensor_scalar(mu, mu, 0.5, None, ALU.mult))
                done(nc.vector.tensor_tensor(diff[:, 0:n], diff[:, 0:n], diff[:, 0:n], ALU.mult))
                done(nc.vector.tensor_scalar(m2[:, 0:n], m2[:, 0:n], 1.0 / D, EPS, ALU.mult, ALU.add))
                own()
                if norm_phase[step]:
                    dve.wait_ge(std_ready, norm_phase[step])
                nc.vector.scalar_tensor_tensor(out=var[:, 0:n], in0=diff[:, 0:n], scalar=0.25, in1=m2[:, 0:n],
                                               op0=ALU.mult, op1=ALU.add).then_inc(var_ready, 1)

            def invert(step):
                use, at = step
                n = norms[step] * R
                dve.wait_ge(std_ready, norm_phase[step] + 1)
                t = slice(at * R, at * R + n)
                done(nc.vector.reciprocal(rstd[use][:, t], std[:, 0:n]))
                own()
                nc.vector.scalar_tensor_tensor(
                    out=offset[use][:, t], in0=mean[use][:, t], scalar=-1.0, in1=rstd[use][:, t],
                    op0=ALU.mult, op1=ALU.mult).then_inc(rstd_ready, 1)
                dve.wait_ge(rstd_ready, norm_phase[step] + 1)

            def normalise(step, others=()):
                variance(step)
                invert(step)
                for c in range(step[1], step[1] + norms[step]):
                    if c not in others:
                        scale(dve, step[0], c)

            def per_expert(ap, w):
                return ap.unsqueeze(1).to_broadcast([P, w, E])

            def pick(k):
                def per_token(ap):
                    return ap.unsqueeze(2).to_broadcast([P, ap.shape[1], E])

                for b, some in enumerate(score_batches(k)):
                    w = some.stop - some.start
                    dve.wait_ge(logits_done, logits_base[k] + some.stop // R)
                    done(nc.vector.tensor_tensor(
                        logits[:, some, :],
                        bank[LOGIT_BANKS[b]][:, 0:w * QUARTER].rearrange("p (t e) -> p t e", e=QUARTER)[:, :, 0:E],
                        per_expert(gate_b_sb[:], w), ALU.add))
                    own()
                    done(nc.vector.tensor_reduce(top[:, some], logits[:, some], AX.X, ALU.max))
                    own()
                    done(nc.vector.tensor_tensor(hit[:, some], logits[:, some], per_token(top[:, some]), ALU.is_ge))
                    own()
                    done(nc.vector.tensor_tensor(hit[:, some], hit[:, some], per_expert(expert_iota, w), ALU.mult))
                    own()
                    done(nc.vector.tensor_reduce(first[:, some], hit[:, some], AX.X, ALU.min))
                    own()
                    nc.vector.tensor_tensor(onehot[:, some], per_expert(expert_iota, w), per_token(first[:, some]),
                                            ALU.is_equal).then_inc(onehot_ready, 1)

            def place_rows(k):
                tg = groups[k][1] * R
                t = slice(0, tg)
                dve.wait_ge(ranks_done, route_phase[k] + 1)
                ranks = bank[RANK_BANK][:, 0:(tg + 1) * E].rearrange("p (t e) -> p t e", e=E)
                done(nc.vector.tensor_scalar(tiles_i[:], ranks[:, tg, :], float(P - 1), None, ALU.add))
                own()
                done(nc.vector.tensor_scalar(tiles_i[:], tiles_i[:], P.bit_length() - 1, None,
                                             ALU.arith_shift_right))
                own()
                done(nc.vector.scalar_tensor_tensor(
                    out=starts_m[:], in0=tiles_i[:].unsqueeze(1).to_broadcast([P, E + 1, E]), scalar=float(LEAST),
                    in1=lower, op0=ALU.max, op1=ALU.mult))
                own()
                done(nc.vector.tensor_reduce(starts_f[:], starts_m[:], AX.X, ALU.add))
                own()
                done(nc.vector.scalar_tensor_tensor(
                    out=place[:, t], in0=per_expert(starts_f[:, 0:E], tg), scalar=float(P), in1=ranks[:, 0:tg, :],
                    op0=ALU.mult, op1=ALU.add))
                done(nc.vector.tensor_copy(starts[k][:], starts_f[:]))
                own()
                done(nc.vector.tensor_tensor(place[:, t], place[:, t], onehot[:, t], ALU.mult))
                own()
                done(nc.vector.tensor_reduce(rows_f[:, t], place[:, t], AX.X, ALU.add))
                own()
                nc.vector.tensor_copy(rows[k][:], rows_f[:, t]).then_inc(routed, 1)

            def experts(k, bounds, between=None):
                dve.wait_ge(halved, 2)
                own()
                if k in early_loaded:
                    dve.wait_ge(early_loaded[k], 16 * EARLY_QUADS)
                    dve.sem_inc(tiles_loaded[k], 16 * EARLY_QUADS)
                dve.sem_inc(y_copied[k], 1)
                dve.sem_inc(relu_v[k], HC // 2)

                tiles_b = tiles[groups[k][2]]

                def stage(i):
                    dve.wait_ge(tiles_loaded[k], 16 * (i // QUAD + 1))
                    nc.vector.tensor_copy(x_stage[:].unsqueeze(1),
                                          tiles_b[:, bass.ds(i, 1), :]).then_inc(x_staged[k], 1)

                def relu(i, e):
                    for c in range(HC // 2, HC):
                        dve.wait_ge(h_done[k], HC * i + c + 1)
                        nc.vector.tensor_scalar(hT[:, c, :], bank[c][:, 0:P],
                                                b1_sb[:, e * HC + c:e * HC + c + 1], 0.0,
                                                ALU.add, ALU.max).then_inc(relu_v[k], 1)
                    dve.wait_ge(xT_done[k], i + 2)
                    stage(i + 2)

                def take_output(following, e):
                    dve.wait_ge(y_done[k], following)
                    nc.vector.tensor_tensor(tiles_b[:, bass.ds(following - 1, 1), :], bank[4][:, 0:D].unsqueeze(1),
                                            b2_sb[:, e:e + 1, :], ALU.add).then_inc(y_copied[k], 1)

                stage(0)
                dve.wait_ge(xT_done[k], 1)
                stage(1)
                relu(0, 0)
                for e in range(E):
                    with dve.Fori(bounds[e] + 1, bounds[e + 1]) as i:
                        take_output(i, e)
                        relu(i, e)
                    take_output(bounds[e + 1], e)
                    if e + 1 < E:
                        relu(bounds[e + 1], e + 1)
                    if between:
                        between(e)
                dve.wait_ge(x_staged[k], bounds[E] + AHEAD)
                dve.sem_inc(v_finished, 1)

            def attn_moments(c):
                dve.wait_ge(ffn_added[c], 1)
                moments("attn", c)

            def first_attn(e):
                lo, hi = [min((i * HEAD + 2) // (FIRST_NORM + 1), HEAD) for i in (e, e + 1)]
                for c in range(lo, hi):
                    attn_moments(c)
                if e == FIRST_NORM:
                    variance(("attn", 0))
                if e == FIRST_NORM + 1:
                    invert(("attn", 0))

            def attention(at, chunks, meanwhile=lambda: None):
                def take_qkv(j):
                    n = at + j
                    dve.wait_ge(qkv_done, n + 1)
                    qkv = bank[1][:, 0:R * QKV].rearrange("p (r n) -> p r n", r=R)
                    nc.vector.tensor_tensor(qk[:].rearrange("p s r n -> p r s n"),
                                            qkv[:, :, 0:2 * CLASS_CH].rearrange("p r (s n) -> p r s n", s=2),
                                            bqkv_sb[:, :, 0:2 * CLASS_CH].rearrange("p r (s n) -> p r s n", s=2),
                                            ALU.add).then_inc(qk_ready, 1)
                    for b in range(2):
                        s = slice(b * SEQ, (b + 1) * SEQ)
                        for h in range(2):
                            col = h * (HEAD_DIM + 1)

                            def pair(ap):
                                return ap[s, :, 2 * CLASS_CH:].rearrange("p r (w h d) -> p r w h d", h=2,
                                                                         d=HEAD_DIM)[:, :, :, h, :]

                            last = nc.vector.tensor_tensor(
                                v_pairs[h * SEQ:(h + 1) * SEQ, n % V_SLOTS, :, :, b, col:col + HEAD_DIM],
                                pair(qkv), pair(bqkv_sb), ALU.add)
                    last.then_inc(v_ready, 1)

                def shift(j):
                    n = at + j
                    for s in range(2):
                        dve.wait_ge(scores_done, 2 * n + s + 1)
                        sc = bank[4 + s][:, :].rearrange("p (h q) -> p h q", q=SEQ)
                        m = row_max[:, 8 * s:8 * s + 8]
                        done(nc.vector.tensor_reduce(m, sc, AX.X, ALU.max))
                        own()
                        nc.vector.tensor_tensor(
                            probs[:, n % 2, 2 * s:2 * s + 2, :].rearrange("p r (h q) -> p (r h) q", q=SEQ), sc,
                            m.unsqueeze(2).to_broadcast([P, 8, SEQ]), ALU.subtract).then_inc(shifted, 1)

                def attend(j):
                    n = at + j
                    dve.wait_ge(ctx_done, n + 1)
                    got = bank[1][:, 0:R * ROWS * PAIR].rearrange("p (w d) -> p w d", d=HEAD_DIM + 1)
                    done(nc.vector.reciprocal(inv_sum[:], got[:, :, HEAD_DIM]))
                    own()
                    nc.vector.tensor_tensor(attended[:], got[:, :, 0:HEAD_DIM],
                                            inv_sum[:].unsqueeze(2).to_broadcast([P, R * CLASS_HEADS, HEAD_DIM]),
                                            ALU.mult).then_inc(ctx_used, 1)
                    dve.wait_ge(ctx_used, n + 1)
                    chunk = x_sb[:, n, :]
                    mine = bass.AP(chunk.tensor, chunk.offset,
                                   [chunk.ap[0], [D + HEAD_DIM, R], [R * HEAD_DIM, CLASS_HEADS], [1, HEAD_DIM]])
                    done(nc.vector.tensor_tensor(mine, mine, attended[:].rearrange("p (r h) d -> p r h d", r=R),
                                                 ALU.add))
                    own()
                    moments("ffn1", n)

                take_qkv(0)
                meanwhile()
                take_qkv(1)
                shift(0)
                for j in range(chunks):
                    if j + 2 < chunks:
                        take_qkv(j + 2)
                    if j + 1 < chunks:
                        shift(j + 1)
                    for step in deviations[at].get(j, ()):
                        invert(step)
                    attend(j)
                    for c in late_moments[at].get(j, ()):
                        attn_moments(c)
                    for step in deviations[at].get(j + 1, ()):
                        variance(step)

            def first_moments(at, chunks):
                for c in range(at, at + chunks):
                    dve.wait_ge(x_loaded[c * XL // CHUNKS], 16)
                    moments("ffn0", c)

            first_moments(0, HEAD)
            normalise(("ffn0", 0), ACT_SCALED.values())
            first_moments(HEAD, EARLY)
            dve.wait_ge(weights_loaded, 64)
            pick((0, 0))
            place_rows((0, 0))
            first_moments(HEAD + EARLY, CHUNKS - HEAD - EARLY)
            normalise(("ffn0", HEAD))
            bounds = expert_bounds(dve, (0, 0))
            pick((0, 1))
            place_rows((0, 1))
            next_bounds = [0]
            experts((0, 0), bounds, lambda e: next_bounds.append(end_of(dve, (0, 1), e)))
            experts((0, 1), next_bounds, first_attn)
            dve.wait_ge(blocks_cleared, 2 + 2 * V_SLOTS)
            attention(*attention_runs[0])
            normalise(("ffn1", HEAD))
            for c in range(MAIN + TAIL // 2, CHUNKS):
                scale(dve, "attn", c)
            pick((1, 0))
            attention(*attention_runs[1], lambda: place_rows((1, 0)))
            normalise(("ffn1", MAIN), ACT_SCALED_LAST.values())
            bounds = expert_bounds(dve, (1, 0))
            pick((1, 1))
            place_rows((1, 1))
            next_bounds = [0]
            experts((1, 0), bounds, lambda e: next_bounds.append(end_of(dve, (1, 1), e)))
            experts((1, 1), next_bounds)
            at, chunks, _ = groups[1, 1]
            for c in range(at, at + chunks):
                add_ffn(dve, 1, c)

        @block.tensor
        def _(pe):
            def transpose_xn(use, c, banks=1):
                n = norm_at[use, c]
                pe.wait_ge(xn_ready[c], norm_round[use])
                if n >= banks:
                    pe.wait_ge(xnT_copied, n + 1 - banks)
                for r in range(R):
                    last = nc.tensor.transpose(bank[n % banks][:, r * P:(r + 1) * P], xn_sb[:, c, r, :], ident)
                last.then_inc(xnT_done, 1)

            def gate(k):
                at, chunks, _ = groups[k]
                use = f"ffn{k[0]}"
                base = norm_at[use, at]
                scored = logits_base[k]
                for j in range(chunks + 2):
                    if j < chunks:
                        transpose_xn(use, at + j, GATE_BANKS)
                    if 1 <= j <= chunks:
                        i = j - 1
                        pe.wait_ge(xnT_copied, base + i + 1)
                        for r in range(R):
                            last = nc.tensor.matmul(bank[LOGIT_T_BANKS[i % 2]][r * QUARTER:(r + 1) * QUARTER, 0:P],
                                                    gate_sb[:], xnT[:, (base + i) % 2, r, :], start=True, stop=True)
                        last.then_inc(logitsT_done, 1)
                    if j >= 2:
                        i = j - 2
                        pe.wait_ge(logitsT_copied, scored + i + 1)
                        nc.tensor.transpose(bank[LOGIT_BANKS[i // 4]][:, i % 4 * P:(i % 4 + 1) * P],
                                            logitsT[:, i % 2, :], ident).then_inc(logits_done, 1)

            def rank(k):
                tg = groups[k][1] * R
                for b, some in enumerate(score_batches(k)):
                    pe.wait_ge(onehot_ready, onehot_base[k] + b + 1)
                    for t in range(some.start, some.stop):
                        later = bank[RANK_BANK][:, (t + 1) * E:(tg + 1) * E].rearrange("p (t e) -> p t e", e=E)
                        last = nc.tensor.matmul(later, ones[:], onehot[:, t:t + 1, :].to_broadcast([P, tg - t, E]),
                                                start=(t == 0), stop=(t == tg - 1), skip_group_check=True)
                        if t == some.start:
                            nc.tensor.matmul(bank[RANK_BANK][:, some.start * E:some.stop * E], tri[:],
                                             onehot[:, some].rearrange("p t e -> p (t e)"),
                                             start=False, stop=False, skip_group_check=True)
                last.then_inc(ranks_done, 1)

            def experts(k, bounds, between=None):
                pe.wait_ge(halved, 2)
                pe.wait_ge(routed, 2 * k[0] + 2)

                def transpose_x(i):
                    pe.wait_ge(x_staged[k], i + 1)
                    nc.tensor.transpose(bank[6][:, 0:P], x_stage[:], ident).then_inc(xT_done[k], 1)

                def hidden(i, e):
                    pe.wait_ge(xT_copied[k], i + 1)
                    for c in range(HC):
                        nc.tensor.matmul(bank[c][:, 0:P], w1_sb[:, e, c * P:(c + 1) * P], xT[:],
                                         start=True, stop=True).then_inc(h_done[k], 1)
                    transpose_x(i + 1)

                def output(following, e):
                    pe.wait_ge(y_copied[k], following)
                    for c in range(HC):
                        pe.wait_ge(relu_a[k] if c < HC // 2 else relu_v[k], HC // 2 * following + c % (HC // 2) + 1)
                        last = nc.tensor.matmul(bank[4][:, 0:D], hT[:, c, :], w2_sb[:, e, c, :],
                                                start=(c == 0), stop=(c == HC - 1))
                    last.then_inc(y_done[k], 1)

                transpose_x(0)
                hidden(0, 0)
                for e in range(E):
                    with pe.Fori(bounds[e] + 1, bounds[e + 1]) as i:
                        output(i, e)
                        hidden(i, e)
                    output(bounds[e + 1], e)
                    if e + 1 < E:
                        hidden(bounds[e + 1], e + 1)
                    if between:
                        between(e)
                pe.wait_ge(xT_copied[k], bounds[E] + 1)
                pe.sem_inc(pe_finished, 1)

            def attention(at, chunks, meanwhile=lambda: None, after=lambda j: None):
                base = norm_at["attn", at]

                def project(j):
                    n = base + j
                    m = at + j
                    pe.wait_ge(xnT_copied, n + 1)
                    if m >= 1:
                        pe.wait_ge(v_ready, m)
                    if j >= 3:
                        pe.wait_ge(ctx_used, m - 2)
                    for r in range(R):
                        last = nc.tensor.matmul(bank[1][:, r * QKV:(r + 1) * QKV], xnT[:, n % 2, r, :],
                                                wqkv_sb[:, r, :], start=True, stop=True)
                    last.then_inc(qkv_done, 1)

                def transpose_qk(j):
                    pe.wait_ge(qk_ready, at + j + 1)
                    for s, done in ((0, qT_done), (1, kT_done)):
                        nc.tensor.transpose(bank[2 + s][:, 0:P], qk[:, s, :, :].rearrange("p r n -> p (r n)"),
                                            ident).then_inc(done, 1)

                def scores(j):
                    n = at + j
                    pe.wait_ge(q_ready, n + 1)
                    pe.wait_ge(k_ready, n + 1)
                    for r in range(R):
                        if n >= 1 and r % 2 == 0:
                            pe.wait_ge(shifted, 2 * n - 1 + r // 2)
                        for b in range(2):
                            s = slice(b * SEQ, (b + 1) * SEQ)
                            last = nc.tensor.matmul(bank[4 + r // 2][s, (r % 2) * 256:(r % 2) * 256 + 256],
                                                    q_by_class[:, r, s], k_by_head[:, :, s], start=True, stop=True)
                        if r % 2:
                            last.then_inc(scores_done, 1)

                def transpose_probs(j):
                    n = at + j
                    for s in range(2):
                        pe.wait_ge(exp_done, 2 * n + s + 1)
                        for u in range(4):
                            r, w = 2 * s + u // 2, u % 2
                            last = nc.tensor.transpose(bank[6 + s][:, u * P:(u + 1) * P],
                                                       probs[:, n % 2, r, w * P:(w + 1) * P], ident)
                        last.then_inc(probsT_done, 1)

                def weigh_values(j):
                    n = at + j
                    pe.wait_ge(v_ready, min(n + 3, at + chunks))
                    if j >= chunks - 2:
                        pe.wait_ge(ctx_used, n)
                    for s in range(2):
                        pe.wait_ge(probsT_copied, 2 * n + s + 1)
                        for u in range(4 * s, 4 * s + 4):
                            for b in range(2):
                                q = slice(b * SEQ, (b + 1) * SEQ)
                                last = nc.tensor.matmul(bank[1][q, u * PAIR:(u + 1) * PAIR], probsT[:, u, q],
                                                        v_pairs[:, n % V_SLOTS, u // ROWS, u % ROWS, b, :],
                                                        start=True, stop=True)
                    last.then_inc(ctx_done, 1)

                transpose_xn("attn", at)
                transpose_xn("attn", at + 1)
                project(0)
                meanwhile()
                transpose_qk(0)
                project(1)
                scores(0)
                transpose_qk(1)
                for j in range(chunks):
                    if j + 2 < chunks:
                        transpose_xn("attn", at + j + 2)
                    if j + 1 < chunks:
                        scores(j + 1)
                    if j + 2 < chunks:
                        project(j + 2)
                    transpose_probs(j)
                    if j + 2 < chunks:
                        transpose_qk(j + 2)
                    weigh_values(j)
                    after(j)
                pe.wait_ge(ctx_used, at + chunks)

            def load_bounds(j):
                for e in range(j * E // TAIL, (j + 1) * E // TAIL):
                    bounds.append(end_of(pe, (1, 0), e))

            pe.wait_ge(consts_loaded, 16)
            pe.wait_ge(weights_loaded, 64)
            gate((0, 0))
            rank((0, 0))
            gate((0, 1))
            rank((0, 1))
            next_bounds = [0]
            experts((0, 0), expert_bounds(pe, (0, 0)), lambda e: next_bounds.append(end_of(pe, (0, 1), e)))
            experts((0, 1), next_bounds)
            pe.wait_ge(blocks_cleared, 2 + 2 * V_SLOTS)
            attention(*attention_runs[0])
            gate((1, 0))
            bounds = [0]
            attention(*attention_runs[1], lambda: rank((1, 0)), load_bounds)
            gate((1, 1))
            rank((1, 1))
            next_bounds = [0]
            experts((1, 0), bounds, lambda e: next_bounds.append(end_of(pe, (1, 1), e)))
            experts((1, 1), next_bounds)


def kernel(L0_attn_X, L0_attn_Wq, L0_attn_bq, L0_attn_Wkv, L0_attn_bkv, L0_ffn_gate_w, L0_ffn_gate_b,
           L0_ffn_w1, L0_ffn_b1, L0_ffn_w2, L0_ffn_b2):
    import concourse.bacc as bacc
    from concourse.bass_utils import run_bass_kernel_spmd

    shape = np.shape(L0_attn_X)
    d = shape[-1]
    e, hid, _ = np.shape(L0_ffn_w1)

    def by_class(w, parts):
        w = np.asarray(w).reshape(-1, parts, CLASS_HEADS, R, HEAD_DIM)
        return w.transpose(0, 3, 1, 2, 4).reshape(-1, R, parts * CLASS_CH)

    arrays = {
        "x": np.asarray(L0_attn_X).reshape(-1, d),
        "w_qkv": np.concatenate([by_class(L0_attn_Wq, 1), by_class(L0_attn_Wkv, 2)], axis=2),
        "b_qkv": np.concatenate([by_class(L0_attn_bq, 1), by_class(L0_attn_bkv, 2)], axis=2)[0],
        "gate_w": np.asarray(L0_ffn_gate_w).T,
        "gate_b": np.asarray(L0_ffn_gate_b),
        "w1": np.asarray(L0_ffn_w1).transpose(2, 0, 1),
        "b1": np.asarray(L0_ffn_b1).reshape(e * hid // P, P).T,
        "w2": np.asarray(L0_ffn_w2).reshape(e, d, hid // P, P).transpose(3, 0, 2, 1),
        "b2": np.asarray(L0_ffn_b2),
        "consts": shape_constants(e),
    }
    nc = bacc.Bacc("TRN2", target_bir_lowering=False, num_devices=1)
    maps, args = {}, []
    for name, a in arrays.items():
        a = np.ascontiguousarray(a)
        maps[f"in_{name}"] = a
        args.append(nc.dram_tensor(f"in_{name}", a.shape, mybir.dt.from_np(a.dtype), kind="ExternalInput").ap())
    args.append(nc.dram_tensor("out_x", arrays["x"].shape, F32, kind="ExternalOutput").ap())
    macaron_kernel(nc, *args)
    got = run_bass_kernel_spmd(nc, [maps], core_ids=[0])
    return got.results[0]["out_x"].reshape(shape)
```
